# Optimizing a Trainium2 kernel written in Bass

```python
import numpy as np
import jax
import jax.numpy as jnp

def _softmax(x, axis=-1):
    return jax.nn.softmax(x, axis=axis)

def _gelu(x):
    return jax.nn.gelu(x, approximate=True)

def _silu(x):
    return jax.nn.silu(x)

def _sigmoid(x):
    return jax.nn.sigmoid(x)

def _layernorm(x, axis=-1, eps=1e-05):
    m = jnp.mean(x, axis=axis, keepdims=True)
    v = jnp.var(x, axis=axis, keepdims=True)
    return (x - m) / jnp.sqrt(v + eps)

def _scatter_add(tgt, idx, src, axis=0):
    return tgt.at[idx].add(src)

def _segment_sum(src, seg, n):
    return jax.ops.segment_sum(src, seg, n)
kernel_name = 'mk_xattn_ffn_d1_seqx_r8_ab7498'

def setup_inputs(seed: int=0):
    np.random.seed(seed)
    _w = jnp.asarray

    def _rec_inputs():
        import jax
        import jax.numpy as jnp
        _rk = jax.random.key(seed)
        x = -0.0003929 + 0.9999 * jax.random.normal(jax.random.fold_in(_rk, 1), (16, 128, 128), jnp.float32)
        _lenS = 128 - jax.random.randint(jax.random.fold_in(_rk, 7), (16,), 0, max(1, 128 // 4) + 1, jnp.int32)
        _lenS2 = 77 - jax.random.randint(jax.random.fold_in(_rk, 8), (16,), 0, max(1, 77 // 4) + 1, jnp.int32)
        _ctx_1024P = jax.random.normal(jax.random.fold_in(_rk, 11), (16, 16, 128), jnp.float32)
        _ctx_1024c = jax.random.dirichlet(jax.random.fold_in(_rk, 511), 0.3 * jnp.ones((16,), jnp.float32), (16, 77))
        _ctx_1024t = jnp.einsum('bsk,bkd->bsd', _ctx_1024c, _ctx_1024P)
        _ctx_1024t = _ctx_1024t * jax.lax.rsqrt(jnp.mean(jnp.square(_ctx_1024t)) + 1e-12) * 0.953939
        ctx_1024 = -3.05549e-07 + 0.0199987 * (_ctx_1024t + 0.3 * jax.random.normal(jax.random.fold_in(_rk, 611), (16, 77, 128), jnp.float32))
        return (x, ctx_1024)
    x, ctx_1024 = _rec_inputs()

    def _L0_xattn_setup():
        import jax, jax.numpy as jnp
        import numpy as np
        E, T, H, F = (8, 256, 128, 512)
        key = jax.random.key(seed)
        k1, k2, k3 = jax.random.split(key, 3)
        x = jax.random.normal(k1, (E, T, H), dtype=jnp.float32)
        w1 = jax.random.normal(k2, (E, F, H), dtype=jnp.float32) * 0.02
        w2 = jax.random.normal(k3, (E, F, H), dtype=jnp.float32) * 0.02
        return {'x': x, 'w1': w1, 'w2': w2}
    _L0_xattn_all = _L0_xattn_setup()
    _L0_xattn_in = {k: v for k, v in _L0_xattn_all.items() if k in ()}
    del _L0_xattn_all

    def _L0_ffn_setup():
        import jax, jax.numpy as jnp
        import numpy as np
        H = 128
        M = 64
        E = 16
        TOP_K = 2
        SCALE = 2.5
        NORM_TOPK = True
        B, S = (1, 128)

        def _moe(x, gate_w, w_gate, w_up, w_down, ws_gate, ws_up, ws_down):
            T = x.shape[0]
            shared = jax.nn.silu(x @ ws_gate) * (x @ ws_up) @ ws_down
            scores = jax.nn.sigmoid(x.astype(jnp.float32) @ gate_w.T.astype(jnp.float32))
            topk_w, topk_idx = jax.lax.top_k(scores, TOP_K)
            if NORM_TOPK and TOP_K > 1:
                topk_w = topk_w / (topk_w.sum(-1, keepdims=True) + 1e-20)
            topk_w = topk_w * SCALE
            route = jnp.zeros((T, E), topk_w.dtype).at[jnp.arange(T)[:, None], topk_idx].set(topk_w)
            g = jnp.einsum('th,ehm->etm', x, w_gate)
            u = jnp.einsum('th,ehm->etm', x, w_up)
            eo = jnp.einsum('etm,emh->eth', jax.nn.silu(g) * u, w_down)
            routed = jnp.einsum('te,eth->th', route.astype(x.dtype), eo)
            return routed + shared
        key = jax.random.key(seed)
        ks = jax.random.split(key, 8)
        std = 0.02
        return {'hidden_states': jax.random.normal(ks[0], (B, S, H), jnp.float32), 'gate_w': jax.random.normal(ks[1], (E, H), jnp.float32) * std, 'w_gate': jax.random.normal(ks[2], (E, H, M), jnp.float32) * std, 'w_up': jax.random.normal(ks[3], (E, H, M), jnp.float32) * std, 'w_down': jax.random.normal(ks[4], (E, M, H), jnp.float32) * std, 'ws_gate': jax.random.normal(ks[5], (H, M), jnp.float32) * std, 'ws_up': jax.random.normal(ks[6], (H, M), jnp.float32) * std, 'ws_down': jax.random.normal(ks[7], (M, H), jnp.float32) * std}
    _L0_ffn_all = _L0_ffn_setup()
    _L0_ffn_in = {k: v for k, v in _L0_ffn_all.items() if k in ('gate_w', 'w_gate', 'w_up', 'w_down', 'ws_gate', 'ws_up', 'ws_down')}
    del _L0_ffn_all
    return {'x': x, 'ctx_1024': ctx_1024, 'L0_ffn_gate_w': _L0_ffn_in['gate_w'], 'L0_ffn_w_gate': _L0_ffn_in['w_gate'], 'L0_ffn_w_up': _L0_ffn_in['w_up'], 'L0_ffn_w_down': _L0_ffn_in['w_down'], 'L0_ffn_ws_gate': _L0_ffn_in['ws_gate'], 'L0_ffn_ws_up': _L0_ffn_in['ws_up'], 'L0_ffn_ws_down': _L0_ffn_in['ws_down']}

def reference(x, ctx_1024, L0_ffn_gate_w, L0_ffn_w_gate, L0_ffn_w_up, L0_ffn_w_down, L0_ffn_ws_gate, L0_ffn_ws_up, L0_ffn_ws_down):
    import jax
    import jax.numpy as jnp

    def _L0_xattn_ref(x, w1, w2):
        import jax, jax.numpy as jnp
        import numpy as np
        E, T, H, F = (8, 256, 128, 512)
        h = jnp.einsum('eth,efh->etf', x, w1)
        a = jax.nn.gelu(h, approximate=True)
        return jnp.einsum('etf,efh->eth', a, w2)

    def _L0_ffn_ref(hidden_states, gate_w, w_gate, w_up, w_down, ws_gate, ws_up, ws_down):
        import jax, jax.numpy as jnp
        import numpy as np
        H = 128
        M = 64
        E = 16
        TOP_K = 2
        SCALE = 2.5
        NORM_TOPK = True
        B, S = (1, 128)

        def _moe(x, gate_w, w_gate, w_up, w_down, ws_gate, ws_up, ws_down):
            T = x.shape[0]
            shared = jax.nn.silu(x @ ws_gate) * (x @ ws_up) @ ws_down
            scores = jax.nn.sigmoid(x.astype(jnp.float32) @ gate_w.T.astype(jnp.float32))
            topk_w, topk_idx = jax.lax.top_k(scores, TOP_K)
            if NORM_TOPK and TOP_K > 1:
                topk_w = topk_w / (topk_w.sum(-1, keepdims=True) + 1e-20)
            topk_w = topk_w * SCALE
            route = jnp.zeros((T, E), topk_w.dtype).at[jnp.arange(T)[:, None], topk_idx].set(topk_w)
            g = jnp.einsum('th,ehm->etm', x, w_gate)
            u = jnp.einsum('th,ehm->etm', x, w_up)
            eo = jnp.einsum('etm,emh->eth', jax.nn.silu(g) * u, w_down)
            routed = jnp.einsum('te,eth->th', route.astype(x.dtype), eo)
            return routed + shared
        b, s, h = hidden_states.shape
        x = hidden_states.reshape(-1, h)
        out = _moe(x, gate_w, w_gate, w_up, w_down, ws_gate, ws_up, ws_down)
        return out.reshape(b, s, h)
    x = x + _L0_xattn_ref(_layernorm(x, axis=-1), ctx_1024, ctx_1024)
    x = x + _L0_ffn_ref(_layernorm(x, axis=-1), L0_ffn_gate_w, L0_ffn_w_gate, L0_ffn_w_up, L0_ffn_w_down, L0_ffn_ws_gate, L0_ffn_ws_up, L0_ffn_ws_down)
    return x

_drawn_inputs = setup_inputs


def setup_inputs(seed=0):
    import zlib

    import numpy as np

    out = dict(_drawn_inputs(seed))
    spreads = {}
    factors = {'L0_ffn_gate_w': 8.0,
     'L0_ffn_w_gate': 7.88,
     'L0_ffn_w_up': 7.844,
     'L0_ffn_w_down': 7.826,
     'L0_ffn_ws_gate': 8.0,
     'L0_ffn_ws_up': 8.0,
     'L0_ffn_ws_down': 8.0}
    for name, (base, spread) in spreads.items():
        noise = np.random.default_rng([zlib.crc32(name.encode()), seed]).standard_normal(out[name].shape)
        drawn = base * np.exp(spread * noise) if base else spread * noise
        out[name] = jnp.asarray(drawn.astype(out[name].dtype))
    for name, factor in factors.items():
        out[name] = (out[name] * factor).astype(out[name].dtype)
    return out
```

```python
from contextlib import ExitStack

import concourse.bass as bass
from concourse import mybir


def xattn_moe_kernel(nc, x, ctx_kv, gate_w, w_gate, w_up, w_down, ws_gate, ws_up, ws_down, out):
    f32 = mybir.dt.float32
    f32r = mybir.dt.float32r
    bf16 = mybir.dt.bfloat16
    ALU = mybir.AluOpType
    ACT = mybir.ActivationFunctionType

    B, S, H = x.shape
    C = ctx_kv.shape[1]
    E, _, M = w_gate.shape
    GB = 4
    NG = B // GB
    T = GB * S
    PAIRS = E // 2
    SLOTS = PAIRS + 1
    ABUF = 4
    EPS = 1e-5
    TOPK_EPS = 1e-20
    ROUTE_SCALE = 2.5
    TOP = 2
    ABSENT = -3.0
    RPARTS = 3
    BN6, BN2 = 6, 2
    MAX8 = 8

    es = ExitStack()
    with es:
        def sb(name, shape, dt):
            return es.enter_context(nc.sbuf_tensor(name, shape, dt))

        def psum(name):
            return es.enter_context(nc.psum_tensor(name, [128, 512], f32))

        def sem(name):
            return es.enter_context(nc.semaphore(name))

        xs = sb("xs", [S, B, H], f32)
        cs = sb("cs", [C, B, H], f32)
        xn1 = sb("xn1", [S, B, H], f32)
        xn1T = sb("xn1T", [H, 2, GB, S], f32)
        csT = sb("csT", [H, 2, GB, C], f32)
        gel = sb("gel", [C, 2, GB, S], f32)
        xn2 = sb("xn2", [S, GB, H], f32)
        xn2T = sb("xn2T", [H, T], f32)
        xH = sb("xH", [H, B * S], f32r)
        xL = sb("xL", [H, B * S], f32r)
        wraw = sb("wraw", [H, 3, E * M], f32)
        wH = sb("wH", [H, 3, E * M], f32r)
        wL = sb("wL", [H, 3, E * M], f32r)
        shraw = sb("shraw", [H, 2 * M], f32)
        shH = sb("shH", [H, 2 * M], f32r)
        shL = sb("shL", [H, 2 * M], f32r)
        shd = sb("shd", [128, H], f32)
        gwr = sb("gwr", [E, H], f32)
        gwT = sb("gwT", [H, E], f32)
        silu_s = sb("silu_s", [128, 2, T], f32)
        gated = sb("gated", [128, 2, T], f32)
        act = sb("act", [128, ABUF, T], f32)
        actH = sb("actH", [128, ABUF, T], f32r)
        actL = sb("actL", [128, ABUF, T], f32r)
        sh_silu = sb("sh_silu", [128, T], f32)
        sh_act = sb("sh_act", [128, T], f32)
        yT = sb("yT", [H, T], f32)
        st1 = sb("st1", [S, B, BN6], f32)
        mv1 = sb("mv1", [S, B, BN2], f32)
        rs1 = sb("rs1", [S, B], f32)
        ve1 = sb("ve1", [S, B], f32)
        nb1 = sb("nb1", [S, B], f32)
        st2 = sb("st2", [S, GB, BN6], f32)
        mv2 = sb("mv2", [S, GB, BN2], f32)
        rs2 = sb("rs2", [S, GB], f32)
        ve2 = sb("ve2", [S, GB], f32)
        epsc = sb("epsc", [S, GB], f32)
        mhalf = sb("mhalf", [S, B], f32)
        SC = E + MAX8 - TOP
        score = sb("score", [S, GB, SC], f32)
        top8 = sb("top8", [S, GB, MAX8], f32)
        top2 = sb("top2", [S, GB, MAX8], f32)
        picked = sb("picked", [S, GB, SC], f32)
        rsum = sb("rsum", [S, GB], f32)
        rinv = sb("rinv", [S, GB], f32)
        r0 = sb("r0", [S, GB, E], f32)
        r1 = sb("r1", [S, GB, E], f32)
        r2 = sb("r2", [S, GB, E], f32)
        r3 = sb("r3", [S, GB, E], f32)
        rparts = sb("rparts", [S, GB, 128], bf16)
        routeT = sb("routeT", [RPARTS * E, T], bf16)
        spread = sb("spread", [RPARTS * E, PAIRS, 2, M], bf16)
        identf = sb("identf", [128, 128], f32)
        identb = sb("identb", [128, 128], bf16)

        pG = [psum("pG0"), psum("pG1")]
        pU = [psum("pU0"), psum("pU1")]
        pR = psum("pR")
        pY = psum("pY")
        pA = psum("pA")
        pB = psum("pB")

        ld_x = [sem(f"ld_x{g}") for g in range(NG)]
        ld_c = [sem(f"ld_c{g}") for g in range(NG)]
        ld_gw = sem("ld_gw")
        ld_sh = sem("ld_sh")
        ld_shd = sem("ld_shd")
        ld_w = [sem(f"ld_w{i}") for i in range(3)]
        pool_seq = sem("pool_seq")
        dve_seq = sem("dve_seq")
        ident_ok = sem("ident_ok")
        spread_ok = sem("spread_ok")
        score_pad = sem("score_pad")
        mv1_ok = sem("mv1_ok")
        rs1_ok = sem("rs1_ok")
        xn1_ok = sem("xn1_ok")
        xn1_ps = sem("xn1_ps")
        ct_ps = sem("ct_ps")
        xn1T_ok = sem("xn1T_ok")
        csT_ok = sem("csT_ok")
        gw_ps = sem("gw_ps")
        gwT_ok = sem("gwT_ok")
        h_ps = sem("h_ps")
        gel_ok = sem("gel_ok")
        att_ps = sem("att_ps")
        x1_ok = sem("x1_ok")
        whi_ok = sem("whi_ok")
        wlo_ok = sem("wlo_ok")
        mv2_ok = sem("mv2_ok")
        rs2_ok = sem("rs2_ok")
        xn2_ok = sem("xn2_ok")
        xn2_ps = sem("xn2_ps")
        xn2T_ok = sem("xn2T_ok")
        xH_ok = sem("xH_ok")
        xL_ok = sem("xL_ok")
        lg_ps = sem("lg_ps")
        score_ok = sem("score_ok")
        rp_ok = sem("rp_ok")
        rt_ps = sem("rt_ps")
        rt_ok = sem("rt_ok")
        gate_ps = sem("gate_ps")
        up_ps = sem("up_ps")
        r_ps = sem("r_ps")
        silu_ok = sem("silu_ok")
        gated_ok = sem("gated_ok")
        act_ok = sem("act_ok")
        actH_ok = sem("actH_ok")
        actL_ok = sem("actL_ok")
        y_ps = sem("y_ps")
        yT_ok = sem("yT_ok")
        yt_ps = sem("yt_ps")
        y_ok = sem("y_ok")
        st_out = sem("st_out")

        xn1T_v = [xn1T[:, i] for i in range(2)]
        csT_v = [csT[:, i] for i in range(2)]
        gel_v = [gel[:, i] for i in range(2)]

        def bcast(ap2, n):
            return ap2.unsqueeze(2).to_broadcast([S, GB, n])

        block = es.enter_context(nc.Block())

        @block.sync
        def _(sp):
            for g in range(NG):
                b0 = g * GB
                sp.dma_start(xs[:, b0:b0 + GB, :], x[b0:b0 + GB].rearrange("b s h -> s b h")).then_inc(ld_x[g], 16)
                sp.dma_start(cs[:, b0:b0 + GB, :], ctx_kv[b0:b0 + GB].rearrange("b s h -> s b h")).then_inc(ld_c[g], 16)
                if g == 0:
                    sp.dma_start(gwr[:, :], gate_w).then_inc(ld_gw, 16)
                    sp.dma_start(shraw[:, 0:M], ws_gate).then_inc(ld_sh, 16)
                    sp.dma_start(shraw[:, M:2 * M], ws_up).then_inc(ld_sh, 16)
                    sp.dma_start(shd[M:2 * M, :], ws_down).then_inc(ld_shd, 16)

            def store(g):
                sp.wait_ge(y_ok, g + 1)
                sp.dma_start(out[bass.ds(g * GB, GB)].rearrange("b s h -> s b h"),
                             xs[:, bass.ds(g * GB, GB), :]).then_inc(st_out, 16)
            with sp.Fori(0, NG) as g:
                store(g)
            sp.wait_ge(st_out, 16 * NG)

        @block.gpsimd
        def _(pool):
            seq = [0]

            def chain(ins):
                seq[0] += 1
                ins.then_inc(pool_seq, 1)
                pool.wait_ge(pool_seq, seq[0])

            chain(pool.memset(identf[:, :], 0.0))
            pool.affine_select(out=identf[:, :], in_=identf[:, :], compare_op=ALU.not_equal, fill=1.0, base=0,
                               pattern=[[-1, 128]], channel_multiplier=1).then_inc(ident_ok, 1)
            pool.memset(epsc[:, :], EPS)
            chain(pool.memset(mhalf[:, :], -0.5))

            def rstd(var, ve, rs, n, ready, at, done):
                pool.wait_ge(ready, at)
                chain(pool.tensor_scalar(ve, var, EPS, None, op0=ALU.add))
                pool.tensor_tensor(rs, ve, mhalf[:, 0:n], ALU.pow).then_inc(done, 1)

            rstd(mv1[:, 0:GB, 1], ve1[:, 0:GB], rs1[:, 0:GB], GB, mv1_ok, 1, rs1_ok)
            chain(pool.memset(identb[:, :], 0.0))
            pool.affine_select(out=identb[:, :], in_=identb[:, :], compare_op=ALU.not_equal, fill=1.0, base=0,
                               pattern=[[-1, 128]], channel_multiplier=1).then_inc(ident_ok, 1)
            pool.wait_ge(mv1_ok, 2)
            chain(pool.tensor_scalar(ve1[:, GB:B], mv1[:, GB:B, 1], EPS, None, op0=ALU.add))
            chain(pool.tensor_tensor(rs1[:, GB:B], ve1[:, GB:B], mhalf[:, GB:B], ALU.pow))
            chain(pool.tensor_tensor(nb1[:, GB:B], mv1[:, GB:B, 0], rs1[:, GB:B], ALU.mult))
            chain(pool.tensor_scalar(nb1[:, GB:B], nb1[:, GB:B], -1.0, None, op0=ALU.mult))
            for g in range(1, NG):
                for b in range(g * GB, (g + 1) * GB):
                    last = pool.tensor_scalar(xn1[:, b, :], xs[:, b, :], rs1[:, b:b + 1], nb1[:, b:b + 1],
                                              op0=ALU.mult, op1=ALU.add)
                last.then_inc(xn1_ok, 1)

            def w_lo(lo, raw, hi, n):
                pool.wait_ge(whi_ok, n)
                pool.tensor_tensor(lo, raw, hi.bitcast(f32), ALU.subtract).then_inc(wlo_ok, 1)

            w_lo(shL[:, :], shraw[:, :], shH[:, :], 1)
            w_lo(wL[:, 0], wraw[:, 0], wH[:, 0], 2)
            w_lo(wL[:, 1], wraw[:, 1], wH[:, 1], 3)

            def x_lo(g):
                pool.wait_ge(xH_ok, g + 1)
                pool.tensor_tensor(xL[:, bass.ds(g * T, T)], xn2T[:, :], xH[:, bass.ds(g * T, T)].bitcast(f32),
                                   ALU.subtract).then_inc(xL_ok, 1)

            def ln2_rstd(g):
                rstd(mv2[:, :, 1], ve2[:, :], rs2[:, :], GB, mv2_ok, g + 1, rs2_ok)

            def act_lo(g, k):
                i = (k - 1) % ABUF
                pool.wait_ge(actH_ok, g * PAIRS + k)
                pool.tensor_tensor(actL[:, i], act[:, i], actH[:, i].bitcast(f32), ALU.subtract).then_inc(actL_ok, 1)

            ln2_rstd(0)
            chain(pool.memset(spread[:, :, :, :], 0.0))
            for c in range(RPARTS):
                last = pool.affine_select(out=spread[:, :, :, :], in_=spread[:, :, :, :], compare_op=ALU.not_equal,
                                          fill=1.0, base=-c * E, pattern=[[-2, PAIRS], [-1, 2], [0, M]],
                                          channel_multiplier=1)
                if c < RPARTS - 1:
                    chain(last)
            last.then_inc(spread_ok, 1)
            x_lo(0)
            w_lo(wL[:, 2], wraw[:, 2], wH[:, 2], 4)
            act_lo(0, 1)

            def slots(g, nxt):
                for k in range(3, SLOTS):
                    act_lo(g, k - 1)
                    if nxt and k == 3:
                        pool_ln2(g + 1)
                    if nxt and k == 5:
                        x_lo(g + 1)
                act_lo(g, SLOTS - 1)
                if nxt:
                    act_lo(g + 1, 1)

            seq_at = seq[0]

            def pool_ln2(g):
                pool.wait_ge(mv2_ok, g + 1)
                pool.tensor_tensor(ve2[:, :], mv2[:, :, 1], epsc[:, :], ALU.add).then_inc(pool_seq, 1)
                pool.wait_ge(pool_seq, g + seq_at)
                pool.tensor_tensor(rs2[:, :], ve2[:, :], mhalf[:, 0:GB], ALU.pow).then_inc(rs2_ok, 1)

            with pool.Fori(0, NG - 1) as g:
                slots(g, True)
            slots(NG - 1, False)

        @block.scalar
        def _(a):
            a.dma_start(wraw[:, 0].rearrange("h (e m) -> h e m", m=M), w_gate.rearrange("e h m -> h e m"))\
                .then_inc(ld_w[0], 16)
            a.dma_start(wraw[:, 1].rearrange("h (e m) -> h e m", m=M), w_up.rearrange("e h m -> h e m"))\
                .then_inc(ld_w[1], 16)
            a.dma_start(wraw[:, 2].rearrange("p (q h) -> p q h", h=H),
                        w_down.rearrange("(q e) m h -> (e m) q h", e=2)).then_inc(ld_w[2], 16)

            def evac(g):
                a.wait_ge(ct_ps, g + 1)
                a.copy(csT_v[g % 2], pU[g % 2][:, 0:GB * C].rearrange("h (b c) -> h b c", c=C)).then_inc(csT_ok, 1)
                a.wait_ge(xn1_ps, g + 1)
                a.copy(xn1T_v[g % 2], pG[g % 2][:, :].rearrange("h (b s) -> h b s", s=S)).then_inc(xn1T_ok, 1)

            def gelu(g):
                a.wait_ge(h_ps, g + 1)
                a.activation(gel_v[g % 2], pY[0:C, :].rearrange("c (b s) -> c b s", s=S),
                             ACT.Gelu_apprx_tanh).then_inc(gel_ok, 1)

            evac(0)
            gelu(0)
            for g in range(1, NG):
                evac(g)
                gelu(g)
                if g == 1:
                    a.wait_ge(gw_ps, 1)
                    a.copy(gwT[:, :], pB[:, 0:E]).then_inc(gwT_ok, 1)
                    a.wait_ge(ld_sh, 32)
                    a.copy(shH[:, :], shraw[:, :]).then_inc(whi_ok, 1)
                    for i in range(2):
                        a.wait_ge(ld_w[i], 16)
                        a.copy(wH[:, i], wraw[:, i]).then_inc(whi_ok, 1)

            def x_hi(g):
                a.wait_ge(xn2T_ok, g + 1)
                a.copy(xH[:, bass.ds(g * T, T)], xn2T[:, :]).then_inc(xH_ok, 1)

            def sigmoid(g):
                a.wait_ge(lg_ps, g + 1)
                a.activation(score[:, :, 0:E], pB[:, 0:GB * E].rearrange("s (b e) -> s b e", e=E),
                             ACT.Sigmoid).then_inc(score_ok, 1)

            def silu(g, k):
                a.wait_ge(gate_ps, g * SLOTS + k + 1)
                if k == 0:
                    a.activation(sh_silu[M:2 * M, :], pU[0][0:M, :], ACT.Silu).then_inc(silu_ok, 1)
                else:
                    i = (k - 1) % 2
                    a.activation(silu_s[:, i], pG[i][:, :], ACT.Silu).then_inc(silu_ok, 1)

            def act_hi(g, k):
                i = (k - 1) % ABUF
                a.wait_ge(act_ok, g * PAIRS + k)
                a.copy(actH[:, i], act[:, i]).then_inc(actH_ok, 1)

            def y_copy(g):
                a.wait_ge(y_ps, g + 1)
                a.copy(yT[:, :], pY[:, :]).then_inc(yT_ok, 1)

            x_hi(0)
            sigmoid(0)
            silu(0, 0)
            silu(0, 1)
            a.wait_ge(ld_w[2], 16)
            a.copy(wH[:, 2], wraw[:, 2]).then_inc(whi_ok, 1)
            act_hi(0, 1)
            silu(0, 2)

            def slots(g, nxt):
                for k in range(3, SLOTS):
                    act_hi(g, k - 1)
                    if nxt and k == 6:
                        sigmoid(g + 1)
                    silu(g, k)
                    if nxt and k == 5:
                        x_hi(g + 1)
                if nxt:
                    act_hi(g, SLOTS - 1)
                    silu(g + 1, 0)
                    silu(g + 1, 1)
                    y_copy(g)
                    act_hi(g + 1, 1)
                    silu(g + 1, 2)
                else:
                    act_hi(g, SLOTS - 1)
                    y_copy(g)

            with a.Fori(0, NG - 1) as g:
                slots(g, True)
            slots(NG - 1, False)

        @block.vector
        def _(v):
            seq = [0]

            def chain(ins, base=None):
                seq[0] += 1
                ins.then_inc(dve_seq, 1)
                v.wait_ge(dve_seq, seq[0] if base is None else base + seq[0])

            v.memset(rparts[:, :, :], 0.0)
            v.memset(score[:, :, E:SC], ABSENT)
            v.memset(top2[:, :, TOP:MAX8], ABSENT).then_inc(score_pad, 1)

            def ln_apply(dst, src, mv, rs):
                return v.tensor_scalar(dst, src, mv, rs, op0=ALU.subtract, op1=ALU.mult)

            def ln1_stats(b0, b1):
                for b in range(b0, b1):
                    if b % GB == 0:
                        v.wait_ge(ld_x[b // GB], 16)
                    last = v.bn_stats(st1[:, b, :], xs[:, b, :])
                chain(last)
                for b in range(b0, b1):
                    last = v.bn_aggr(mv1[:, b, :], st1[:, b, :])
                last.then_inc(mv1_ok, 1)

            ln1_stats(0, GB)
            v.wait_ge(rs1_ok, 1)
            v.wait_ge(mv1_ok, 1)
            for b in range(GB):
                last = ln_apply(xn1[:, b, :], xs[:, b, :], mv1[:, b, 0:1], rs1[:, b:b + 1])
            last.then_inc(xn1_ok, 1)
            ln1_stats(GB, B)

            def residual(g):
                v.wait_ge(att_ps, g + 1)
                sl = xs[:, g * GB:(g + 1) * GB, :]
                v.tensor_tensor(sl, pR[:, :].rearrange("s (b h) -> s b h", h=H), sl, ALU.add).then_inc(x1_ok, 1)

            def ln2_stats(g, ch):
                for b in range(GB):
                    last = v.bn_stats(st2[:, b, :], xs[:, bass.ds(g * GB + b, 1), :])
                ch(last)

            def ln2_aggregate():
                for b in range(GB):
                    last = v.bn_aggr(mv2[:, b, :], st2[:, b, :])
                last.then_inc(mv2_ok, 1)

            def ln2_apply(g):
                v.wait_ge(rs2_ok, g + 1)
                for b in range(GB):
                    last = ln_apply(xn2[:, b, :], xs[:, bass.ds(g * GB + b, 1), :], mv2[:, b, 0:1], rs2[:, b:b + 1])
                last.then_inc(xn2_ok, 1)

            def ln2_evac(g):
                v.wait_ge(xn2_ps, g + 1)
                v.tensor_copy(xn2T[:, :], pA[:, :]).then_inc(xn2T_ok, 1)

            def route_a(g, ch):
                for b in range(GB):
                    last = v.max(top8[:, b, :], score[:, b, 0:E])
                ch(last)
                ch(v.tensor_copy(top2[:, :, 0:TOP], top8[:, :, 0:TOP]))
                v.scalar_tensor_tensor(rsum[:, :], top8[:, :, 0], TOPK_EPS, top8[:, :, 1], op0=ALU.add, op1=ALU.add)
                for b in range(GB):
                    last = v.match_replace(picked[:, b, :], top2[:, b, :], score[:, b, :], ABSENT)
                ch(last)
                v.reciprocal(rinv[:, :], rsum[:, :])
                ch(v.tensor_scalar(r0[:, :, :], picked[:, :, 0:E], 0.0, ROUTE_SCALE, op0=ALU.is_lt, op1=ALU.mult))

            def route_b(g, ch):
                ch(v.tensor_tensor(r1[:, :, :], score[:, :, 0:E], r0[:, :, :], ALU.mult))
                ch(v.tensor_tensor(r2[:, :, :], r1[:, :, :], bcast(rinv[:, :], E), ALU.mult))
                ch(v.tensor_copy(rparts[:, :, 0:E], r2[:, :, :]))
                ch(v.tensor_tensor(r3[:, :, :], r2[:, :, :], rparts[:, :, 0:E], ALU.subtract))
                ch(v.tensor_copy(rparts[:, :, E:2 * E], r3[:, :, :]))
                v.tensor_tensor(rparts[:, :, 2 * E:3 * E], r3[:, :, :], rparts[:, :, E:2 * E],
                                ALU.subtract).then_inc(rp_ok, 1)

            def route_evac(g):
                v.wait_ge(rt_ps, g + 1)
                v.tensor_copy(routeT[:, :], pA[0:RPARTS * E, 0:T // 2].bitcast(bf16)).then_inc(rt_ok, 1)

            def gate_up(g, k):
                v.wait_ge(silu_ok, g * SLOTS + k + 1)
                if k == 0:
                    v.tensor_tensor(sh_act[M:2 * M, :], pU[0][M:2 * M, :], sh_silu[M:2 * M, :],
                                    ALU.mult).then_inc(gated_ok, 1)
                else:
                    i = (k - 1) % 2
                    v.wait_ge(up_ps, g * PAIRS + k)
                    v.tensor_tensor(gated[:, i], pU[i][:, :], silu_s[:, i], ALU.mult).then_inc(gated_ok, 1)

            def apply_route(g, k):
                i, j = (k - 1) % 2, (k - 1) % ABUF
                v.wait_ge(r_ps, g * PAIRS + k)
                v.wait_ge(gated_ok, g * SLOTS + k + 1)
                v.tensor_tensor(act[:, j], pR[:, :], gated[:, i], ALU.mult).then_inc(act_ok, 1)

            def out_add(g):
                v.wait_ge(yt_ps, g + 1)
                sl = xs[:, bass.ds(g * GB, GB), :]
                v.tensor_tensor(sl, pB[:, :].rearrange("s (b h) -> s b h", h=H), sl, ALU.add).then_inc(y_ok, 1)

            residual(0)
            v.wait_ge(x1_ok, 1)
            ln2_stats(0, chain)
            ln2_aggregate()
            residual(1)
            ln2_apply(0)
            residual(2)
            ln2_evac(0)
            residual(3)
            v.wait_ge(score_pad, 1)
            v.wait_ge(score_ok, 1)
            route_a(0, chain)
            route_b(0, chain)
            gate_up(0, 0)
            route_evac(0)
            gate_up(0, 1)
            apply_route(0, 1)
            gate_up(0, 2)
            apply_route(0, 2)
            v.wait_ge(x1_ok, NG)
            before = seq[0]
            PER = 10

            def slots(g, nxt):
                seq[0] = before

                def ch(ins):
                    chain(ins, g * PER)
                for k in range(3, SLOTS):
                    if nxt and k == 3:
                        ln2_stats(g + 1, ch)
                    if nxt and k == 4:
                        ln2_apply(g + 1)
                    if nxt and k == 5:
                        ln2_evac(g + 1)
                    if nxt and k == 7:
                        route_a(g + 1, ch)
                    if nxt and k == 8:
                        route_b(g + 1, ch)
                        assert seq[0] == before + PER, seq[0] - before
                    if nxt and k == 6:
                        v.wait_ge(score_ok, g + 2)
                    gate_up(g, k)
                    if nxt and k == 3:
                        ln2_aggregate()
                    apply_route(g, k)
                if nxt:
                    gate_up(g + 1, 0)
                    route_evac(g + 1)
                    gate_up(g + 1, 1)
                    apply_route(g + 1, 1)
                    gate_up(g + 1, 2)
                    apply_route(g + 1, 2)
                out_add(g)

            with v.Fori(0, NG - 1) as g:
                slots(g, True)
            slots(NG - 1, False)

        @block.tensor
        def _(pe):
            def transposes1(g):
                pe.wait_ge(ld_c[g], 16)
                if g >= 2:
                    pe.wait_ge(csT_ok, g - 1)
                    pe.wait_ge(xn1T_ok, g - 1)
                for b in range(GB):
                    last = pe.transpose(pU[g % 2][:, b * C:(b + 1) * C], cs[:, g * GB + b, :], identf[0:C, 0:C])
                last.then_inc(ct_ps, 1)
                pe.wait_ge(xn1_ok, g + 1)
                for b in range(GB):
                    last = pe.transpose(pG[g % 2][:, b * S:(b + 1) * S], xn1[:, g * GB + b, :], identf[:, :])
                last.then_inc(xn1_ps, 1)

            def attend(g):
                pe.wait_ge(csT_ok, g + 1)
                pe.wait_ge(xn1T_ok, g + 1)
                if g >= 1:
                    pe.wait_ge(gel_ok, g)
                for b in range(GB):
                    last = pe.matmul(pY[0:C, b * S:(b + 1) * S], csT_v[g % 2][:, b, :], xn1T_v[g % 2][:, b, :],
                                     start=True, stop=True)
                last.then_inc(h_ps, 1)

            def attend_out(g):
                pe.wait_ge(gel_ok, g + 1)
                if g >= 1:
                    pe.wait_ge(x1_ok, g)
                for b in range(GB):
                    last = pe.matmul(pR[:, b * H:(b + 1) * H], gel_v[g % 2][:, b, :], cs[:, g * GB + b, :],
                                     start=True, stop=True)
                last.then_inc(att_ps, 1)

            def ln2_transposes(g):
                pe.wait_ge(xn2_ok, g + 1)
                for b in range(GB):
                    last = pe.transpose(pA[:, b * S:(b + 1) * S], xn2[:, b, :], identf[:, :])
                last.then_inc(xn2_ps, 1)

            def logits(g):
                pe.wait_ge(xn2T_ok, g + 1)
                for b in range(GB):
                    last = pe.matmul(pB[:, b * E:(b + 1) * E], xn2T[:, b * S:(b + 1) * S], gwT[:, :],
                                     start=True, stop=True)
                last.then_inc(lg_ps, 1)

            def route_transposes(g):
                pe.wait_ge(rp_ok, g + 1)
                pAb = pA[:, 0:T // 2].bitcast(bf16)
                for b in range(GB):
                    last = pe.transpose(pAb[:, b * S:(b + 1) * S], rparts[:, b, :], identb[:, :])
                last.then_inc(rt_ps, 1)

            def three(dst, hi, lo, g):
                th, tl = xH[:, bass.ds(g * T, T)], xL[:, bass.ds(g * T, T)]
                pe.matmul(dst, hi, th, start=True, stop=False)
                pe.matmul(dst, hi, tl, start=False, stop=False)
                return pe.matmul(dst, lo, th, start=False, stop=True)

            def up_gate(g, k, waits=True):
                if k == 0:
                    if waits:
                        pe.wait_ge(gated_ok, g * SLOTS - 1)
                    pe.wait_ge(xL_ok, g + 1)
                    three(pU[0][:, :], shH[:, :], shL[:, :], g).then_inc(gate_ps, 1)
                    return
                q, i = k - 1, (k - 1) % 2
                c0 = q * 2 * M
                if k >= 2:
                    pe.wait_ge(gated_ok, g * SLOTS + k - 1)
                three(pG[i][:, :], wH[:, 0, c0:c0 + 2 * M], wL[:, 0, c0:c0 + 2 * M], g).then_inc(gate_ps, 1)
                if k == 1:
                    pe.wait_ge(gated_ok, g * SLOTS + 1)
                three(pU[i][:, :], wH[:, 1, c0:c0 + 2 * M], wL[:, 1, c0:c0 + 2 * M], g).then_inc(up_ps, 1)

            def spread_route(g, k, waits=True):
                if k == 1:
                    pe.wait_ge(rt_ok, g + 1)
                if waits:
                    pe.wait_ge(act_ok, g * PAIRS + k - 1)
                pe.matmul(pR[:, :], spread[:, k - 1].rearrange("e a m -> e (a m)"), routeT[:, :],
                          start=True, stop=True).then_inc(r_ps, 1)

            def down(g, k, waits=True):
                if k == 0:
                    pe.wait_ge(gated_ok, g * SLOTS + 1)
                    if waits:
                        pe.wait_ge(yT_ok, g)
                    pe.matmul(pY[:, :], shd[M:2 * M, :], sh_act[M:2 * M, :], start=True, stop=False)
                    return
                i, c0 = (k - 1) % ABUF, (k - 1) * H
                dH, dL = wH[:, 2, c0:c0 + H], wL[:, 2, c0:c0 + H]
                pe.wait_ge(actH_ok, g * PAIRS + k)
                pe.matmul(pY[:, :], dH, actH[:, i], start=False, stop=False)
                pe.matmul(pY[:, :], dL, actH[:, i], start=False, stop=False)
                pe.wait_ge(actL_ok, g * PAIRS + k)
                last = pe.matmul(pY[:, :], dH, actL[:, i], start=False, stop=(k == SLOTS - 1))
                if k == SLOTS - 1:
                    last.then_inc(y_ps, 1)

            def out_transposes(g):
                pe.wait_ge(yT_ok, g + 1)
                for b in range(GB):
                    last = pe.transpose(pB[:, b * H:(b + 1) * H], yT[:, b * S:(b + 1) * S], identf[:, :])
                last.then_inc(yt_ps, 1)

            pe.wait_ge(ident_ok, 1)
            transposes1(0)
            attend(0)
            transposes1(1)
            attend_out(0)
            pe.wait_ge(ld_gw, 16)
            pe.transpose(pB[:, 0:E], gwr[:, :], identf[0:E, 0:E]).then_inc(gw_ps, 1)
            attend(1)
            transposes1(2)
            attend_out(1)
            attend(2)
            transposes1(3)
            attend_out(2)
            ln2_transposes(0)
            attend(3)
            pe.wait_ge(gwT_ok, 1)
            logits(0)
            attend_out(3)
            pe.wait_ge(ident_ok, 2)
            pe.wait_ge(spread_ok, 1)
            pe.wait_ge(wlo_ok, 1)
            up_gate(0, 0, waits=False)
            route_transposes(0)
            pe.wait_ge(wlo_ok, 3)
            up_gate(0, 1)
            pe.wait_ge(x1_ok, NG)
            spread_route(0, 1, waits=False)
            up_gate(0, 2)
            spread_route(0, 2)
            pe.wait_ge(ld_shd, 16)
            down(0, 0, waits=False)
            pe.wait_ge(wlo_ok, 4)

            def slots(g, nxt):
                for k in range(3, SLOTS):
                    up_gate(g, k)
                    spread_route(g, k)
                    if nxt and k == 4:
                        ln2_transposes(g + 1)
                    if nxt and k == 5:
                        logits(g + 1)
                    if nxt and k == 8:
                        route_transposes(g + 1)
                    down(g, k - 2)
                if nxt:
                    up_gate(g + 1, 0)
                    down(g, SLOTS - 2)
                    up_gate(g + 1, 1)
                    spread_route(g + 1, 1)
                    down(g, SLOTS - 1)
                    up_gate(g + 1, 2)
                    spread_route(g + 1, 2)
                    out_transposes(g)
                    down(g + 1, 0)
                else:
                    down(g, SLOTS - 2)
                    down(g, SLOTS - 1)
                    out_transposes(g)

            with pe.Fori(0, NG - 1) as g:
                slots(g, True)
            slots(NG - 1, False)


_INS = ["x", "ctx_1024", "L0_ffn_gate_w", "L0_ffn_w_gate", "L0_ffn_w_up", "L0_ffn_w_down", "L0_ffn_ws_gate",
        "L0_ffn_ws_up", "L0_ffn_ws_down"]
_OUT = (16, 128, 128)


def kernel(**inputs):
    import numpy as np
    import concourse.bacc as bacc
    from concourse import mybir as mb
    from concourse.bass_utils import run_bass_kernel_spmd

    nc = bacc.Bacc("TRN2", target_bir_lowering=False, num_devices=1)
    arrays, args = {}, []
    for name in _INS:
        a = np.ascontiguousarray(inputs[name])
        arrays[f"in_{name}_dram"] = a
        args.append(nc.dram_tensor(f"in_{name}_dram", a.shape, mb.dt.from_np(a.dtype), kind="ExternalInput").ap())
    args.append(nc.dram_tensor("out_dram", _OUT, mb.dt.float32, kind="ExternalOutput").ap())
    xattn_moe_kernel(nc, *args)
    r = run_bass_kernel_spmd(nc, [arrays], core_ids=[0])
    return r.results[0]["out_dram"]
```

```python
from contextlib import ExitStack

import concourse.bass as bass
from concourse import mybir


def xattn_moe_kernel(nc, x, ctx_kv, ctx_t, gate_t, w_gate, w_up, w_down, ws_gu, ws_down, eye, eye16, spread01, out):
    f32 = mybir.dt.float32
    f32r = mybir.dt.float32r
    bf16 = mybir.dt.bfloat16
    ALU = mybir.AluOpType
    ACT = mybir.ActivationFunctionType

    S, B, H = x.shape
    C = ctx_kv.shape[0]
    E, M = gate_t.shape[1], ws_down.shape[0]
    GB = 4
    NG = B // GB
    T = GB * S
    PAIRS = E // 2
    SLOTS = PAIRS + 1
    WARM = [14, 2, 1, 2, 2, 2]
    LAG = 3
    ABUF = 4
    EPS = 1e-5
    TOPK_EPS = 1e-20
    ROUTE_SCALE = 2.5
    TOP = 2
    ABSENT = -3.0
    RPARTS = 3
    BN6, BN2 = 6, 2
    MAX8 = 8

    es = ExitStack()
    with es:
        def sb(name, shape, dt):
            return es.enter_context(nc.sbuf_tensor(name, shape, dt))

        def psum(name):
            return es.enter_context(nc.psum_tensor(name, [128, 512], f32))

        def sem(name):
            return es.enter_context(nc.semaphore(name))

        xs = sb("xs", [S, B, H], f32)
        cs = sb("cs", [C, B, H], f32)
        xn1 = sb("xn1", [S, B, H], f32)
        xn1T = sb("xn1T", [H, 2, GB, S], f32)
        csT = sb("csT", [H, B, C], f32)
        gel = sb("gel", [C, 2, GB, S], f32)
        xn2 = sb("xn2", [S, GB, H], f32)
        xn2T = sb("xn2T", [H, T], f32)
        xH = sb("xH", [H, B * S], f32r)
        xL = sb("xL", [H, B * S], f32r)
        wraw = sb("wraw", [H, 3, E * M], f32)
        wH = sb("wH", [H, 3, E * M], f32r)
        wL = sb("wL", [H, 3, E * M], f32r)
        shraw = sb("shraw", [H, 2 * M], f32)
        shH = sb("shH", [H, 2 * M], f32r)
        shL = sb("shL", [H, 2 * M], f32r)
        shd = sb("shd", [128, H], f32)
        gwT = sb("gwT", [H, E], f32)
        silu_s = sb("silu_s", [128, 2, T], f32)
        gated = sb("gated", [128, 2, T], f32)
        act = sb("act", [128, ABUF, T], f32)
        actH = sb("actH", [128, ABUF, T], f32r)
        actL = sb("actL", [128, ABUF, T], f32r)
        sh_silu = sb("sh_silu", [128, T], f32)
        sh_act = sb("sh_act", [128, T], f32)
        yT = sb("yT", [H, T], f32)
        st1 = sb("st1", [S, B, BN6], f32)
        mv1 = sb("mv1", [S, B, BN2], f32)
        rs1 = sb("rs1", [S, B], f32)
        ve1 = sb("ve1", [S, B], f32)
        nb1 = sb("nb1", [S, B], f32)
        st2 = sb("st2", [S, GB, BN6], f32)
        mv2 = sb("mv2", [S, GB, BN2], f32)
        rs2 = sb("rs2", [S, GB], f32)
        ve2 = sb("ve2", [S, GB], f32)
        epsc = sb("epsc", [S, GB], f32)
        mhalf = sb("mhalf", [S, B], f32)
        SC = E + MAX8 - TOP
        score = sb("score", [S, GB, SC], f32)
        top8 = sb("top8", [S, GB, MAX8], f32)
        top2 = sb("top2", [S, GB, MAX8], f32)
        picked = sb("picked", [S, GB, SC], f32)
        rsum = sb("rsum", [S, GB], f32)
        rinv = sb("rinv", [S, GB], f32)
        r1 = sb("r1", [S, GB, E], f32)
        r2 = sb("r2", [S, GB, E], f32)
        r3 = sb("r3", [S, GB, E], f32)
        rparts = sb("rparts", [S, GB, 128], bf16)
        routeT = sb("routeT", [RPARTS * E, T], bf16)
        spread = sb("spread", [RPARTS * E, PAIRS, 2, M], bf16)
        warm = sb("warm", [128, T // 2], f32)
        identf = sb("identf", [128, 128], f32)
        identb = sb("identb", [128, 128], bf16)

        pG = [psum("pG0"), psum("pG1")]
        pU = [psum("pU0"), psum("pU1")]
        pR = [psum("pR0"), psum("pR1")]
        pY = psum("pY")
        pA = psum("pA")

        ld_x = [sem(f"ld_x{g}") for g in range(NG)]
        ld_c0 = sem("ld_c0")
        ld_c = sem("ld_c")
        ld_ct0 = sem("ld_ct0")
        ld_ct = sem("ld_ct")
        ld_gw = sem("ld_gw")
        ld_eye = sem("ld_eye")
        ld_eye16 = sem("ld_eye16")
        ld_spread = sem("ld_spread")
        ld_sh = sem("ld_sh")
        ld_shd = sem("ld_shd")
        ld_w = [sem(f"ld_w{i}") for i in range(3)]
        pool_seq = sem("pool_seq")
        dve_seq = sem("dve_seq")
        score_pad = sem("score_pad")
        warm_in = sem("warm_in")
        mv1_ok = sem("mv1_ok")
        rs1_ok = sem("rs1_ok")
        nb1_ok = sem("nb1_ok")
        xn1_ok = sem("xn1_ok")
        xn1a_ok = sem("xn1a_ok")
        xn1_ps = sem("xn1_ps")
        xn1T_ok = sem("xn1T_ok")
        h_ps = sem("h_ps")
        gel_ok = sem("gel_ok")
        att_ps = sem("att_ps")
        x1_ok = sem("x1_ok")
        whi_ok = sem("whi_ok")
        wlo_ok = sem("wlo_ok")
        mv2_ok = sem("mv2_ok")
        rs2_ok = sem("rs2_ok")
        xn2_ok = sem("xn2_ok")
        xn2_ps = sem("xn2_ps")
        xn2T_ok = sem("xn2T_ok")
        xH_ok = sem("xH_ok")
        xL_ok = sem("xL_ok")
        lg_ps = sem("lg_ps")
        score_ok = sem("score_ok")
        rp_ok = sem("rp_ok")
        rt_ps = sem("rt_ps")
        rt_ok = sem("rt_ok")
        gate_ps = sem("gate_ps")
        up_ps = sem("up_ps")
        r_ps = sem("r_ps")
        silu_ok = sem("silu_ok")
        gated_ok = sem("gated_ok")
        act_ok = sem("act_ok")
        actH_ok = sem("actH_ok")
        actL_ok = sem("actL_ok")
        y_ps = sem("y_ps")
        yT_ok = sem("yT_ok")
        yt_ps = sem("yt_ps")
        y_ok = sem("y_ok")
        st_out = sem("st_out")

        xn1T_v = [xn1T[:, i] for i in range(2)]
        gel_v = [gel[:, i] for i in range(2)]

        def sh_bank(g):
            return pU[1] if isinstance(g, int) and g == 0 else pU[0]

        def bcast(ap2, n):
            return ap2.unsqueeze(2).to_broadcast([S, GB, n])

        block = es.enter_context(nc.Block())

        @block.sync
        def _(sp):
            def load_x(b0, b1, done):
                sp.dma_start(xs[:, b0:b1, :], x[:, b0:b1, :]).then_inc(done, 16)

            load_x(0, GB, ld_x[0])
            load_x(GB, 2 * GB, ld_x[1])
            sp.dma_start(identf[:, :], eye).then_inc(ld_eye, 16)
            sp.dma_start(csT[:, 0:GB, :], ctx_t[:, 0:GB, :]).then_inc(ld_ct0, 16)
            load_x(2 * GB, 3 * GB, ld_x[2])
            sp.dma_start(cs[:, 0:GB, :], ctx_kv[:, 0:GB, :]).then_inc(ld_c0, 16)
            sp.dma_start(shraw[:, :], ws_gu).then_inc(ld_sh, 16)
            load_x(3 * GB, B, ld_x[3])
            sp.dma_start(wraw[:, 0], w_gate).then_inc(ld_w[0], 16)
            sp.dma_start(csT[:, GB:B, :], ctx_t[:, GB:B, :]).then_inc(ld_ct, 16)
            sp.dma_start(cs[:, GB:B, :], ctx_kv[:, GB:B, :]).then_inc(ld_c, 16)
            sp.dma_start(wraw[:, 1], w_up).then_inc(ld_w[1], 16)
            sp.dma_start(gwT[:, :], gate_t).then_inc(ld_gw, 16)
            sp.dma_start(identb[:, :], eye16).then_inc(ld_eye16, 16)
            sp.dma_start(spread[:, :, :, :], spread01).then_inc(ld_spread, 16)
            sp.dma_start(wraw[:, 2], w_down).then_inc(ld_w[2], 16)
            sp.dma_start(shd[M:2 * M, :], ws_down).then_inc(ld_shd, 16)

            def store(g):
                sp.wait_ge(y_ok, g + 1)
                sp.dma_start(out[:, bass.ds(g * GB, GB), :], xs[:, bass.ds(g * GB, GB), :]).then_inc(st_out, 16)
            with sp.Fori(0, NG) as g:
                store(g)
            sp.wait_ge(st_out, 16 * NG)

        @block.gpsimd
        def _(pool):
            seq = [0]

            def chain(ins):
                seq[0] += 1
                ins.then_inc(pool_seq, 1)
                pool.wait_ge(pool_seq, seq[0])

            pool.memset(epsc[:, :], EPS)
            chain(pool.memset(mhalf[:, :], -0.5))

            def rstd(var, ve, rs, n, ready, at, done):
                pool.wait_ge(ready, at)
                chain(pool.tensor_scalar(ve, var, EPS, None, op0=ALU.add))
                pool.tensor_tensor(rs, ve, mhalf[:, 0:n], ALU.pow).then_inc(done, 1)

            for g in range(NG):
                b0, b1 = g * GB, (g + 1) * GB
                rstd(mv1[:, b0:b1, 1], ve1[:, b0:b1], rs1[:, b0:b1], GB, mv1_ok, g + 1, rs1_ok)
                if g == 2:
                    pool.wait_ge(rs1_ok, g + 1)
                    chain(pool.tensor_tensor(nb1[:, b0:b1], mv1[:, b0:b1, 0], rs1[:, b0:b1], ALU.mult))
                    pool.tensor_scalar(nb1[:, b0:b1], nb1[:, b0:b1], -1.0, None, op0=ALU.mult).then_inc(nb1_ok, 1)

            def w_lo(lo, raw, hi, n):
                pool.wait_ge(whi_ok, n)
                pool.tensor_tensor(lo, raw, hi.bitcast(f32), ALU.subtract).then_inc(wlo_ok, 1)

            def x_lo(g):
                pool.wait_ge(xH_ok, g + 1)
                pool.tensor_tensor(xL[:, bass.ds(g * T, T)], xn2T[:, :], xH[:, bass.ds(g * T, T)].bitcast(f32),
                                   ALU.subtract).then_inc(xL_ok, 1)

            def ln2_rstd(g):
                rstd(mv2[:, :, 1], ve2[:, :], rs2[:, :], GB, mv2_ok, g + 1, rs2_ok)

            def act_lo(g, k):
                i = (k - 1) % ABUF
                pool.wait_ge(actH_ok, g * PAIRS + k)
                pool.tensor_tensor(actL[:, i], act[:, i], actH[:, i].bitcast(f32), ALU.subtract).then_inc(actL_ok, 1)

            w_lo(shL[:, :], shraw[:, :], shH[:, :], 1)
            ln2_rstd(0)
            w_lo(wL[:, 0], wraw[:, 0], wH[:, 0], 2)
            w_lo(wL[:, 1], wraw[:, 1], wH[:, 1], 3)
            w_lo(wL[:, 2], wraw[:, 2], wH[:, 2], 4)
            act_lo(0, 1)

            def slots(g, nxt):
                for k in range(3, SLOTS):
                    act_lo(g, k - 1)
                    if nxt and k == 3:
                        pool_ln2(g + 1)
                    if nxt and k == 6:
                        x_lo(g + 1)
                if nxt:
                    act_lo(g, SLOTS - 1)
                    act_lo(g + 1, 1)

            seq_at = seq[0]

            def pool_ln2(g):
                pool.wait_ge(mv2_ok, g + 1)
                pool.tensor_tensor(ve2[:, :], mv2[:, :, 1], epsc[:, :], ALU.add).then_inc(pool_seq, 1)
                pool.wait_ge(pool_seq, g + seq_at)
                pool.tensor_tensor(rs2[:, :], ve2[:, :], mhalf[:, 0:GB], ALU.pow).then_inc(rs2_ok, 1)

            with pool.Fori(0, NG - 1) as g:
                slots(g, True)
            slots(NG - 1, False)

        @block.scalar
        def _(a):
            a.wait_ge(warm_in, 1)
            a.activation(gel[0:C, 0, 0, 0:1], warm[0:C, 0:1], ACT.Gelu_apprx_tanh)

            def evac(g):
                a.wait_ge(xn1_ps, g + 1)
                a.copy(xn1T_v[g % 2], pG[g % 2][:, :].rearrange("h (b s) -> h b s", s=S)).then_inc(xn1T_ok, 1)

            def gelu(g):
                a.wait_ge(h_ps, g + 1)
                a.activation(gel_v[g % 2], pU[g % 2][0:C, :].rearrange("c (b s) -> c b s", s=S),
                             ACT.Gelu_apprx_tanh).then_inc(gel_ok, 1)

            def w_hi(hi, raw, loaded):
                a.wait_ge(loaded, 16)
                a.copy(hi, raw).then_inc(whi_ok, 1)

            def x_hi(g):
                a.wait_ge(xn2T_ok, g + 1)
                a.copy(xH[:, bass.ds(g * T, T)], xn2T[:, :]).then_inc(xH_ok, 1)

            def sigmoid(g):
                a.wait_ge(lg_ps, g + 1)
                a.activation(score[:, :, 0:E], pA[:, 0:GB * E].rearrange("s (b e) -> s b e", e=E),
                             ACT.Sigmoid).then_inc(score_ok, 1)

            def silu(g, k):
                a.wait_ge(gate_ps, g * SLOTS + k + 1)
                if k == 0:
                    a.activation(sh_silu[M:2 * M, :], sh_bank(g)[0:M, :], ACT.Silu).then_inc(silu_ok, 1)
                else:
                    i = (k - 1) % 2
                    a.activation(silu_s[:, i], pG[i][:, :], ACT.Silu).then_inc(silu_ok, 1)

            def act_hi(g, k):
                i = (k - 1) % ABUF
                a.wait_ge(act_ok, g * PAIRS + k)
                a.copy(actH[:, i], act[:, i]).then_inc(actH_ok, 1)

            def y_copy(g):
                a.wait_ge(y_ps, g + 1)
                a.copy(yT[:, :], pY[:, :]).then_inc(yT_ok, 1)

            evac(0)
            w_hi(shH[:, :], shraw[:, :], ld_sh)
            w_hi(wH[:, 0], wraw[:, 0], ld_w[0])
            gelu(0)
            evac(1)
            a.wait_ge(nb1_ok, 1)
            for b in range(2 * GB, 3 * GB):
                a.activation(xn1[:, b, :], xs[:, b, :], ACT.Identity, bias=nb1[:, b:b + 1],
                             scale=rs1[:, b:b + 1]).then_inc(xn1a_ok, 1)
            gelu(1)
            evac(2)
            w_hi(wH[:, 1], wraw[:, 1], ld_w[1])
            gelu(2)
            evac(3)
            x_hi(0)
            gelu(3)
            sigmoid(0)
            silu(0, 0)
            silu(0, 1)
            w_hi(wH[:, 2], wraw[:, 2], ld_w[2])
            silu(0, 2)
            act_hi(0, 1)

            def slots(g, nxt):
                for k in range(3, SLOTS):
                    silu(g, k)
                    act_hi(g, k - 1)
                    if nxt and k == 6:
                        x_hi(g + 1)
                        sigmoid(g + 1)
                if nxt:
                    silu(g + 1, 0)
                    act_hi(g, SLOTS - 1)
                    silu(g + 1, 1)
                    y_copy(g)
                    silu(g + 1, 2)
                    act_hi(g + 1, 1)
                else:
                    y_copy(g)

            with a.Fori(0, NG - 1) as g:
                slots(g, True)
            slots(NG - 1, False)

        @block.vector
        def _(v):
            seq = [0]

            def chain(ins, base=None):
                seq[0] += 1
                ins.then_inc(dve_seq, 1)
                v.wait_ge(dve_seq, seq[0] if base is None else base + seq[0])

            v.memset(warm[:, :], 0.0).then_inc(warm_in, 1)
            v.memset(rparts[:, :, :], 0.0)
            v.memset(score[:, :, E:SC], ABSENT)
            v.memset(top2[:, :, TOP:MAX8], ABSENT).then_inc(score_pad, 1)

            def ln_apply(dst, src, mv, rs):
                return v.tensor_scalar(dst, src, mv, rs, op0=ALU.subtract, op1=ALU.mult)

            def ln1_stats(b0, b1):
                for b in range(b0, b1):
                    if b % GB == 0:
                        v.wait_ge(ld_x[b // GB], 16)
                    last = v.bn_stats(st1[:, b, :], xs[:, b, :])
                chain(last)
                for b in range(b0, b1):
                    last = v.bn_aggr(mv1[:, b, :], st1[:, b, :])
                last.then_inc(mv1_ok, 1)

            def ln1_apply(g):
                v.wait_ge(mv1_ok, g + 1)
                v.wait_ge(rs1_ok, g + 1)
                for b in range(g * GB, (g + 1) * GB):
                    ln_apply(xn1[:, b, :], xs[:, b, :], mv1[:, b, 0:1], rs1[:, b:b + 1]).then_inc(xn1_ok, 1)

            ln1_stats(0, GB)
            ln1_stats(GB, 2 * GB)
            ln1_apply(0)
            ln1_stats(2 * GB, 3 * GB)
            ln1_apply(1)
            ln1_stats(3 * GB, B)

            def residual(g):
                v.wait_ge(att_ps, g + 1)
                sl = xs[:, g * GB:(g + 1) * GB, :]
                v.tensor_tensor(sl, pR[g % 2][:, :].rearrange("s (b h) -> s b h", h=H), sl, ALU.add).then_inc(x1_ok, 1)

            def ln2_stats(g, ch):
                for b in range(GB):
                    last = v.bn_stats(st2[:, b, :], xs[:, bass.ds(g * GB + b, 1), :])
                ch(last)

            def ln2_aggregate():
                for b in range(GB):
                    last = v.bn_aggr(mv2[:, b, :], st2[:, b, :])
                last.then_inc(mv2_ok, 1)

            def ln2_apply(g):
                v.wait_ge(rs2_ok, g + 1)
                for b in range(GB):
                    ln_apply(xn2[:, b, :], xs[:, bass.ds(g * GB + b, 1), :], mv2[:, b, 0:1],
                             rs2[:, b:b + 1]).then_inc(xn2_ok, 1)

            def ln2_evac(g):
                v.wait_ge(xn2_ps, g + 1)
                v.tensor_copy(xn2T[:, :], pA[:, :]).then_inc(xn2T_ok, 1)

            def route_a(g, ch):
                v.wait_ge(score_pad, 1)
                v.wait_ge(score_ok, g + 1)
                for b in range(GB):
                    last = v.max(top8[:, b, :], score[:, b, 0:E])
                ch(last)
                ch(v.tensor_copy(top2[:, :, 0:TOP], top8[:, :, 0:TOP]))
                v.scalar_tensor_tensor(rsum[:, :], top8[:, :, 0], TOPK_EPS, top8[:, :, 1], op0=ALU.add, op1=ALU.add)
                for b in range(GB):
                    last = v.match_replace(picked[:, b, :], top2[:, b, :], score[:, b, :], ABSENT)
                ch(last)

            def route_b(g, ch):
                v.reciprocal(rinv[:, :], rsum[:, :])
                ch(v.scalar_tensor_tensor(r1[:, :, :], picked[:, :, 0:E], 0.0, score[:, :, 0:E],
                                          op0=ALU.is_lt, op1=ALU.mult))
                part = [rparts[:, :, c * E:(c + 1) * E] for c in range(RPARTS)]
                v.scalar_tensor_tensor(part[0], r1[:, :, :], ROUTE_SCALE, bcast(rinv[:, :], E),
                                       op0=ALU.mult, op1=ALU.mult)
                ch(v.scalar_tensor_tensor(r2[:, :, :], r1[:, :, :], ROUTE_SCALE, bcast(rinv[:, :], E),
                                          op0=ALU.mult, op1=ALU.mult))
                v.tensor_tensor(part[1], r2[:, :, :], part[0], ALU.subtract)
                ch(v.tensor_tensor(r3[:, :, :], r2[:, :, :], part[0], ALU.subtract))
                v.tensor_tensor(part[2], r3[:, :, :], part[1], ALU.subtract).then_inc(rp_ok, 1)

            def route_evac(g):
                v.wait_ge(rt_ps, g + 1)
                v.tensor_copy(routeT[:, :], pA[0:RPARTS * E, 0:T // 2].bitcast(bf16)).then_inc(rt_ok, 1)

            def gate_up(g, k):
                v.wait_ge(silu_ok, g * SLOTS + k + 1)
                if k == 0:
                    v.tensor_tensor(sh_act[M:2 * M, :], sh_bank(g)[M:2 * M, :], sh_silu[M:2 * M, :],
                                    ALU.mult).then_inc(gated_ok, 1)
                else:
                    i = (k - 1) % 2
                    v.wait_ge(up_ps, g * PAIRS + k)
                    v.tensor_tensor(gated[:, i], pU[i][:, :], silu_s[:, i], ALU.mult).then_inc(gated_ok, 1)

            def apply_route(g, k):
                i, j = (k - 1) % 2, (k - 1) % ABUF
                v.wait_ge(r_ps, g * PAIRS + k)
                v.wait_ge(gated_ok, g * SLOTS + k + 1)
                v.tensor_tensor(act[:, j], pR[i][:, :], gated[:, i], ALU.mult).then_inc(act_ok, 1)

            def out_add(g):
                v.wait_ge(yt_ps, g + 1)
                sl = xs[:, bass.ds(g * GB, GB), :]
                v.tensor_tensor(sl, pA[:, :].rearrange("s (b h) -> s b h", h=H), sl, ALU.add).then_inc(y_ok, 1)

            residual(0)
            v.wait_ge(x1_ok, 1)
            ln2_stats(0, chain)
            ln2_aggregate()
            ln1_apply(3)
            ln2_apply(0)
            ln2_evac(0)
            residual(1)
            v.wait_ge(xH_ok, 1)
            v.tensor_tensor(xL[:, 0:T], xn2T[:, :], xH[:, 0:T].bitcast(f32), ALU.subtract).then_inc(xL_ok, 1)
            residual(2)
            route_a(0, chain)
            route_b(0, chain)
            gate_up(0, 0)
            route_evac(0)
            residual(3)
            gate_up(0, 1)
            apply_route(0, 1)
            gate_up(0, 2)
            apply_route(0, 2)
            v.wait_ge(x1_ok, NG)
            before = seq[0]
            PER = 7

            def slots(g, nxt):
                seq[0] = before

                def ch(ins):
                    chain(ins, g * PER)
                for k in range(3, SLOTS):
                    if nxt and k == 3:
                        ln2_stats(g + 1, ch)
                    if nxt and k == 7:
                        route_a(g + 1, ch)
                        route_b(g + 1, ch)
                        assert seq[0] == before + PER, seq[0] - before
                    gate_up(g, k)
                    if nxt and k == 3:
                        ln2_aggregate()
                    if nxt and k == 4:
                        ln2_apply(g + 1)
                    if nxt and k == 5:
                        ln2_evac(g + 1)
                    if nxt and k == 8:
                        route_evac(g + 1)
                    apply_route(g, k)
                if nxt:
                    gate_up(g + 1, 0)
                    gate_up(g + 1, 1)
                    apply_route(g + 1, 1)
                    gate_up(g + 1, 2)
                    apply_route(g + 1, 2)
                out_add(g)

            with v.Fori(0, NG - 1) as g:
                slots(g, True)
            slots(NG - 1, False)

        @block.tensor
        def _(pe):
            def transposes1(g):
                if g >= 2:
                    pe.wait_ge(xn1T_ok, g - 1)
                for b in range(GB):
                    if g == 2:
                        pe.wait_ge(xn1a_ok, b + 1)
                    else:
                        pe.wait_ge(xn1_ok, (g if g < 2 else 2) * GB + b + 1)
                    last = pe.transpose(pG[g % 2][:, b * S:(b + 1) * S], xn1[:, g * GB + b, :], identf[:, :])
                last.then_inc(xn1_ps, 1)

            def attend(g):
                if g <= 1:
                    pe.wait_ge(ld_ct if g else ld_ct0, 16)
                pe.wait_ge(xn1T_ok, g + 1)
                if g >= 2:
                    pe.wait_ge(gel_ok, g - 1)
                for b in range(GB):
                    last = pe.matmul(pU[g % 2][0:C, b * S:(b + 1) * S], csT[:, g * GB + b, :],
                                     xn1T_v[g % 2][:, b, :], start=True, stop=True)
                last.then_inc(h_ps, 1)

            def attend_out(g):
                if g <= 1:
                    pe.wait_ge(ld_c if g else ld_c0, 16)
                pe.wait_ge(gel_ok, g + 1)
                if g >= 2:
                    pe.wait_ge(x1_ok, g - 1)
                for b in range(GB):
                    last = pe.matmul(pR[g % 2][:, b * H:(b + 1) * H], gel_v[g % 2][:, b, :], cs[:, g * GB + b, :],
                                     start=True, stop=True)
                last.then_inc(att_ps, 1)

            def ln2_transposes(g):
                for b in range(GB):
                    pe.wait_ge(xn2_ok, g * GB + b + 1)
                    last = pe.transpose(pA[:, b * S:(b + 1) * S], xn2[:, b, :], identf[:, :])
                last.then_inc(xn2_ps, 1)

            def logits(g):
                pe.wait_ge(xn2T_ok, g + 1)
                for b in range(GB):
                    last = pe.matmul(pA[:, b * E:(b + 1) * E], xn2T[:, b * S:(b + 1) * S], gwT[:, :],
                                     start=True, stop=True)
                last.then_inc(lg_ps, 1)

            def route_transposes(g):
                pe.wait_ge(rp_ok, g + 1)
                pAb = pA[:, 0:T // 2].bitcast(bf16)
                for b in range(GB):
                    last = pe.transpose(pAb[:, b * S:(b + 1) * S], rparts[:, b, :], identb[:, :])
                last.then_inc(rt_ps, 1)

            def three(dst, hi, lo, g):
                th, tl = xH[:, bass.ds(g * T, T)], xL[:, bass.ds(g * T, T)]
                pe.matmul(dst, hi, th, start=True, stop=False)
                pe.matmul(dst, hi, tl, start=False, stop=False)
                return pe.matmul(dst, lo, th, start=False, stop=True)

            def up_gate(g, k, waits=True, between=None, route=True):
                if k == 0:
                    if waits:
                        pe.wait_ge(gated_ok, g * SLOTS - 1)
                    pe.wait_ge(xL_ok, g + 1)
                    three(sh_bank(g)[:, :], shH[:, :], shL[:, :], g).then_inc(gate_ps, 1)
                    return
                q, i = k - 1, (k - 1) % 2
                c0 = q * 2 * M
                if k >= 2 and waits:
                    pe.wait_ge(gated_ok, g * SLOTS + k - 1)
                three(pG[i][:, :], wH[:, 0, c0:c0 + 2 * M], wL[:, 0, c0:c0 + 2 * M], g).then_inc(gate_ps, 1)
                if k == 1 and route:
                    spread_route(g, k, waits)
                if between:
                    between()
                if k == 1 and route:
                    pe.wait_ge(gated_ok, g * SLOTS + 1)
                three(pU[i][:, :], wH[:, 1, c0:c0 + 2 * M], wL[:, 1, c0:c0 + 2 * M], g).then_inc(up_ps, 1)
                if k > 1:
                    spread_route(g, k, waits)

            def spread_route(g, k, waits=True):
                if k == 1:
                    pe.wait_ge(rt_ok, g + 1)
                if waits:
                    pe.wait_ge(act_ok, g * PAIRS + k - 2)
                else:
                    pe.wait_ge(x1_ok, NG - 2 + k)
                pe.matmul(pR[(k - 1) % 2][:, :], spread[:, k - 1].rearrange("e a m -> e (a m)"), routeT[:, :],
                          start=True, stop=True).then_inc(r_ps, 1)

            def down(g, k, waits=True, direct=False):
                if k == 0:
                    pe.wait_ge(gated_ok, g * SLOTS + 1)
                    pe.matmul(pY[:, :], shd[M:2 * M, :], sh_act[M:2 * M, :], start=True, stop=False)
                    return
                i, c0 = (k - 1) % ABUF, (k - 1) * H
                if direct:
                    pe.wait_ge(act_ok, g * PAIRS + k)
                    pe.matmul(pY[:, :], wraw[:, 2, c0:c0 + H], act[:, i], start=False, stop=True).then_inc(y_ps, 1)
                    return
                dH, dL = wH[:, 2, c0:c0 + H], wL[:, 2, c0:c0 + H]
                pe.wait_ge(actH_ok, g * PAIRS + k)
                pe.matmul(pY[:, :], dH, actH[:, i], start=False, stop=False)
                pe.matmul(pY[:, :], dL, actH[:, i], start=False, stop=False)
                pe.wait_ge(actL_ok, g * PAIRS + k)
                last = pe.matmul(pY[:, :], dH, actL[:, i], start=False, stop=(k == SLOTS - 1))
                if k == SLOTS - 1:
                    last.then_inc(y_ps, 1)

            def out_transposes(g):
                pe.wait_ge(yT_ok, g + 1)
                for b in range(GB):
                    last = pe.transpose(pA[:, b * H:(b + 1) * H], yT[:, b * S:(b + 1) * S], identf[:, :])
                last.then_inc(yt_ps, 1)

            zero16 = warm[:, :].bitcast(bf16)

            def keep_warm(n):
                for _ in range(n):
                    pe.matmul(pY[:, :], zero16[:, 0:128], zero16, start=True, stop=True)

            pe.wait_ge(warm_in, 1)
            keep_warm(WARM[0])
            pe.wait_ge(ld_eye, 16)
            transposes1(0)
            keep_warm(WARM[1])
            attend(0)
            transposes1(1)
            keep_warm(WARM[2])
            attend_out(0)
            attend(1)
            keep_warm(WARM[3])
            transposes1(2)
            attend_out(1)
            attend(2)
            transposes1(3)
            attend_out(2)
            ln2_transposes(0)
            attend(3)
            pe.wait_ge(ld_gw, 16)
            logits(0)
            keep_warm(WARM[4])
            pe.wait_ge(wlo_ok, 1)
            pe.wait_ge(gel_ok, NG)
            up_gate(0, 0, waits=False)
            attend_out(3)
            pe.wait_ge(wlo_ok, 3)
            up_gate(0, 1, waits=False, route=False)
            pe.wait_ge(ld_eye16, 16)
            route_transposes(0)
            keep_warm(WARM[5])
            pe.wait_ge(ld_spread, 16)
            spread_route(0, 1, waits=False)
            pe.wait_ge(gated_ok, 1)
            up_gate(0, 2, waits=False)
            pe.wait_ge(ld_shd, 16)
            pe.wait_ge(wlo_ok, 4)

            def slots(g, nxt):
                for k in range(3, SLOTS):
                    up_gate(g, k, between=(lambda: logits(g + 1)) if nxt and k == 6 else None)
                    if nxt and k == 5:
                        ln2_transposes(g + 1)
                    if nxt and k == 8:
                        route_transposes(g + 1)
                    down(g, k - LAG)
                if nxt:
                    up_gate(g + 1, 0)
                    down(g, SLOTS - 3)
                    up_gate(g + 1, 1, between=lambda: down(g, SLOTS - 2))
                    down(g, SLOTS - 1)
                    up_gate(g + 1, 2)
                    out_transposes(g)
                else:
                    down(g, SLOTS - 3)
                    down(g, SLOTS - 2)
                    down(g, SLOTS - 1, direct=True)
                    out_transposes(g)

            with pe.Fori(0, NG - 1) as g:
                slots(g, True)
            slots(NG - 1, False)


def kernel(x, ctx_1024, L0_ffn_gate_w, L0_ffn_w_gate, L0_ffn_w_up, L0_ffn_w_down, L0_ffn_ws_gate, L0_ffn_ws_up,
           L0_ffn_ws_down):
    import ml_dtypes
    import numpy as np
    import concourse.bacc as bacc
    from concourse import mybir as mb
    from concourse.bass_utils import run_bass_kernel_spmd

    x, ctx = np.asarray(x), np.asarray(ctx_1024)
    w_gate, w_up, w_down = (np.asarray(w) for w in (L0_ffn_w_gate, L0_ffn_w_up, L0_ffn_w_down))
    E, H, M = w_gate.shape
    PARTS = 3
    spread01 = np.tile(np.repeat(np.eye(E), M, axis=1), (PARTS, 1)).reshape(PARTS * E, E // 2, 2, M)
    laid_out = {
        "x": x.transpose(1, 0, 2),
        "ctx_kv": ctx.transpose(1, 0, 2),
        "ctx_t": ctx.transpose(2, 0, 1),
        "gate_t": np.asarray(L0_ffn_gate_w).T,
        "w_gate": w_gate.transpose(1, 0, 2).reshape(H, E * M),
        "w_up": w_up.transpose(1, 0, 2).reshape(H, E * M),
        "w_down": w_down.reshape(E // 2, 2 * M, H).transpose(1, 0, 2).reshape(2 * M, E // 2 * H),
        "ws_gu": np.concatenate([np.asarray(L0_ffn_ws_gate), np.asarray(L0_ffn_ws_up)], axis=1),
        "ws_down": np.asarray(L0_ffn_ws_down),
        "eye": np.eye(128, dtype=np.float32),
        "eye16": np.eye(128).astype(ml_dtypes.bfloat16),
        "spread01": spread01.astype(ml_dtypes.bfloat16),
    }
    nc = bacc.Bacc("TRN2", target_bir_lowering=False, num_devices=1)
    arrays, args = {}, []
    for name, a in laid_out.items():
        a = np.ascontiguousarray(a)
        arrays[f"in_{name}"] = a
        args.append(nc.dram_tensor(f"in_{name}", a.shape, mb.dt.from_np(a.dtype), kind="ExternalInput").ap())
    B, S, _ = x.shape
    args.append(nc.dram_tensor("out_dram", (S, B, H), mb.dt.float32, kind="ExternalOutput").ap())
    xattn_moe_kernel(nc, *args)
    r = run_bass_kernel_spmd(nc, [arrays], core_ids=[0])
    return r.results[0]["out_dram"].transpose(1, 0, 2)
```

```python
from contextlib import ExitStack

import concourse.bass as bass
from concourse import mybir


def xattn_moe_kernel(nc, x, ctx_kv, ctx_t, gate_t, w_gate, w_up, w_down, ws_gu, ws_down, eye, eye16, spread01, out):
    f32 = mybir.dt.float32
    f32r = mybir.dt.float32r
    bf16 = mybir.dt.bfloat16
    ALU = mybir.AluOpType
    ACT = mybir.ActivationFunctionType

    S, B, H = x.shape
    C = ctx_kv.shape[0]
    E, M = gate_t.shape[1], ws_down.shape[0]
    GB = 4
    HB = GB // 2
    NG = B // GB
    T = GB * S
    PAIRS = E // 2
    SLOTS = PAIRS + 1
    WARM = [14, 2, 1, 2, 2, 1, 2]
    LAG = 4
    GBUF = 4
    ABUF = 8
    EPS = 1e-5
    TOPK_EPS = 1e-20
    ROUTE_SCALE = 2.5
    TOP = 2
    TINY = 1e-20
    SATURATED = 16.64
    ABSENT = -3.0
    RPARTS = 3
    BN6, BN2 = 6, 2
    MAX8 = 8

    es = ExitStack()
    with es:
        def sb(name, shape, dt):
            return es.enter_context(nc.sbuf_tensor(name, shape, dt))

        def psum(name):
            return es.enter_context(nc.psum_tensor(name, [128, 512], f32))

        def sem(name):
            return es.enter_context(nc.semaphore(name))

        xs = sb("xs", [S, B + GB, H], f32)
        cs = sb("cs", [C, B, H], f32)
        xn1 = sb("xn1", [S, B, H], f32)
        xn1T = sb("xn1T", [H, 2, GB, S], f32)
        csT = sb("csT", [H, B, C], f32)
        gel = sb("gel", [C, 2, GB, S], f32)
        xn2 = sb("xn2", [S, GB, H], f32)
        xn2T = sb("xn2T", [H, T], f32)
        xH = sb("xH", [H, B * S], f32r)
        xL = sb("xL", [H, B * S], f32r)
        wraw = sb("wraw", [H, 3, E * M], f32)
        wH = sb("wH", [H, 3, E * M], f32r)
        wL = sb("wL", [H, 3, E * M], f32r)
        shraw = sb("shraw", [H, 2 * M], f32)
        shH = sb("shH", [H, 2 * M], f32r)
        shL = sb("shL", [H, 2 * M], f32r)
        shd = sb("shd", [128, H], f32)
        shdH = sb("shdH", [128, H], f32r)
        shdL = sb("shdL", [128, H], f32r)
        gwT = sb("gwT", [H, E], f32)
        silu_s = sb("silu_s", [128, 2, T], f32)
        gated = sb("gated", [128, GBUF, T], f32)
        act = sb("act", [128, ABUF, T], f32)
        actH = sb("actH", [128, ABUF, T], f32r)
        actL = sb("actL", [128, ABUF, T], f32r)
        sh_silu = sb("sh_silu", [128, T], f32)
        sh_act = sb("sh_act", [128, T], f32)
        sh_parts = sb("sh_parts", [128, T], f32r)
        yT = sb("yT", [H, T], f32)
        st1 = sb("st1", [S, B, BN6], f32)
        mv1 = sb("mv1", [S, B, BN2], f32)
        ve1 = sb("ve1", [S, B], f32)
        rs1 = sb("rs1", [S, B], f32)
        nb1 = sb("nb1", [S, B], f32)
        st2 = sb("st2", [S, GB, BN6], f32)
        mv2 = sb("mv2", [S, GB, BN2], f32)
        ve2 = sb("ve2", [S, GB], f32)
        rs2 = sb("rs2", [S, GB], f32)
        nm2 = sb("nm2", [S, GB], f32)
        nb2 = sb("nb2", [S, GB], f32)
        epsc = sb("epsc", [S, GB], f32)
        minus1 = sb("minus1", [S, GB], f32)
        mhalf = sb("mhalf", [S, GB], f32)
        SC = E + MAX8 - TOP
        above = sb("above", [S, GB, E], f32)
        near0 = sb("near0", [S, GB, E], f32)
        logit = sb("logit", [S, GB, E], f32)
        logit_c = sb("logit_c", [S, GB, E], f32)
        logit_r = sb("logit_r", [S, GB, E], f32)
        logit_silu = sb("logit_silu", [S, GB, E], f32)
        score = sb("score", [S, GB, SC], f32)
        top8 = sb("top8", [S, GB, MAX8], f32)
        top2 = sb("top2", [S, GB, MAX8], f32)
        picked = sb("picked", [S, GB, SC], f32)
        rsum = sb("rsum", [S, GB], f32)
        rinv = sb("rinv", [S, GB], f32)
        r1 = sb("r1", [S, GB, E], f32)
        r2 = sb("r2", [S, GB, E], f32)
        r3 = sb("r3", [S, GB, E], f32)
        rparts = sb("rparts", [S, GB, 128], bf16)
        routeT = sb("routeT", [RPARTS * E, T], bf16)
        spread = sb("spread", [RPARTS * E, PAIRS, 2, M], bf16)
        warm = sb("warm", [128, T // 2], f32)
        identf = sb("identf", [128, 128], f32)
        identb = sb("identb", [128, 128], bf16)

        pG = [psum("pG0"), psum("pG1")]
        pU = [psum("pU0"), psum("pU1")]
        pR = [psum("pR0"), psum("pR1")]
        pY = psum("pY")
        pA = psum("pA")

        ld_x_half = sem("ld_x_half")
        ld_x = [sem(f"ld_x{g}") for g in range(NG)]
        ld_c0 = sem("ld_c0")
        ld_c = sem("ld_c")
        ld_ct0 = sem("ld_ct0")
        ld_ct = sem("ld_ct")
        ld_gw = sem("ld_gw")
        ld_eye = sem("ld_eye")
        ld_eye16 = sem("ld_eye16")
        ld_spread = sem("ld_spread")
        ld_sh = sem("ld_sh")
        ld_shd = sem("ld_shd")
        ld_w = [sem(f"ld_w{i}") for i in range(3)]
        pool_seq = sem("pool_seq")
        dve_seq = sem("dve_seq")
        score_pad = sem("score_pad")
        warm_in = sem("warm_in")
        mv1_ok = sem("mv1_ok")
        rs1_ok = sem("rs1_ok")
        nb1_ok = sem("nb1_ok")
        xn1_ok = sem("xn1_ok")
        xn1a_ok = sem("xn1a_ok")
        xn1_ps = sem("xn1_ps")
        xn1T_ok = sem("xn1T_ok")
        h_ps = sem("h_ps")
        gel_ok = sem("gel_ok")
        att_ps = sem("att_ps")
        x1_ok = sem("x1_ok")
        whi_ok = sem("whi_ok")
        wlo_ok = sem("wlo_ok")
        pad_ok = sem("pad_ok")
        mv2_ok = sem("mv2_ok")
        rs2_ok = sem("rs2_ok")
        nb2_ok = sem("nb2_ok")
        xn2_ok = sem("xn2_ok")
        xn2_ps = sem("xn2_ps")
        xn2T_ok = sem("xn2T_ok")
        xH_ok = sem("xH_ok")
        xL_ok = sem("xL_ok")
        lg_ps = sem("lg_ps")
        logit_ok = sem("logit_ok")
        lsilu_ok = sem("lsilu_ok")
        score_ok = sem("score_ok")
        rp_ok = sem("rp_ok")
        rt_ps = sem("rt_ps")
        rt_ok = sem("rt_ok")
        gate_ps = sem("gate_ps")
        up_ps = sem("up_ps")
        r_ps = sem("r_ps")
        silu_ok = sem("silu_ok")
        gated_ok = sem("gated_ok")
        act_ok = sem("act_ok")
        shaH_ok = sem("shaH_ok")
        shaL_ok = sem("shaL_ok")
        actH_ok = sem("actH_ok")
        actL_ok = sem("actL_ok")
        y_ps = sem("y_ps")
        yT_ok = sem("yT_ok")
        yt_ps = sem("yt_ps")
        y_ok = sem("y_ok")
        st_out = sem("st_out")

        y_last = [pA, pG[0], pU[0], pR[0]]
        xn1T_v = [xn1T[:, i] for i in range(2)]
        gel_v = [gel[:, i] for i in range(2)]

        def sh_bank(first):
            return pU[1] if first else pU[0]

        def bcast(ap2, n):
            return ap2.unsqueeze(2).to_broadcast([S, GB, n])

        block = es.enter_context(nc.Block())

        @block.sync
        def _(sp):
            def load_x(b0, b1, done):
                sp.dma_start(xs[:, b0:b1, :], x[:, b0:b1, :]).then_inc(done, 16)

            load_x(0, GB // 2, ld_x_half)
            load_x(GB // 2, GB, ld_x[0])
            load_x(GB, 2 * GB, ld_x[1])
            sp.dma_start(identf[:, :], eye).then_inc(ld_eye, 16)
            sp.dma_start(csT[:, 0:GB, :], ctx_t[:, 0:GB, :]).then_inc(ld_ct0, 16)
            load_x(2 * GB, 3 * GB, ld_x[2])
            sp.dma_start(cs[:, 0:GB, :], ctx_kv[:, 0:GB, :]).then_inc(ld_c0, 16)
            sp.dma_start(shraw[:, :], ws_gu).then_inc(ld_sh, 16)
            load_x(3 * GB, B, ld_x[3])
            sp.dma_start(wraw[:, 0], w_gate).then_inc(ld_w[0], 16)
            sp.dma_start(csT[:, GB:B, :], ctx_t[:, GB:B, :]).then_inc(ld_ct, 16)
            sp.dma_start(cs[:, GB:B, :], ctx_kv[:, GB:B, :]).then_inc(ld_c, 16)
            sp.dma_start(wraw[:, 1], w_up).then_inc(ld_w[1], 16)
            sp.dma_start(gwT[:, :], gate_t).then_inc(ld_gw, 16)
            sp.dma_start(identb[:, :], eye16).then_inc(ld_eye16, 16)
            sp.dma_start(spread[:, :, :, :], spread01).then_inc(ld_spread, 16)
            sp.dma_start(wraw[:, 2], w_down).then_inc(ld_w[2], 16)
            sp.dma_start(shd[0:M, :], ws_down).then_inc(ld_shd, 16)
            sp.dma_start(shd[M:2 * M, :], ws_down).then_inc(ld_shd, 16)

            with sp.Fori(0, NG - 1) as g:
                sp.wait_ge(y_ok, g + 1)
                sp.dma_start(out[:, bass.ds(g * GB, GB), :], xs[:, bass.ds(g * GB, GB), :]).then_inc(st_out, 16)
            for half in range(2):
                b0 = (NG - 1) * GB + half * HB
                sp.wait_ge(y_ok, NG + half)
                sp.dma_start(out[:, b0:b0 + HB, :], xs[:, b0:b0 + HB, :]).then_inc(st_out, 16)
            sp.wait_ge(st_out, 16 * (NG + 1))

        @block.gpsimd
        def _(pool):
            seq = [0]

            def chain(ins):
                seq[0] += 1
                ins.then_inc(pool_seq, 1)
                pool.wait_ge(pool_seq, seq[0])

            pool.memset(epsc[:, :], EPS)
            pool.memset(minus1[:, :], -1.0)
            pool.memset(xs[:, B:B + GB, :], 0.0).then_inc(pad_ok, 1)
            chain(pool.memset(mhalf[:, :], -0.5))

            for g in range(NG):
                b0, b1 = g * GB, (g + 1) * GB
                pool.wait_ge(mv1_ok, g + 1)
                chain(pool.tensor_scalar(ve1[:, b0:b1], mv1[:, b0:b1, 1], EPS, None, op0=ALU.add))
                pool.tensor_tensor(rs1[:, b0:b1], ve1[:, b0:b1], mhalf[:, :], ALU.pow).then_inc(rs1_ok, 1)
                if g == 2:
                    pool.wait_ge(rs1_ok, g + 1)
                    chain(pool.tensor_tensor(nb1[:, b0:b1], mv1[:, b0:b1, 0], rs1[:, b0:b1], ALU.mult))
                    pool.tensor_scalar(nb1[:, b0:b1], nb1[:, b0:b1], -1.0, None, op0=ALU.mult).then_inc(nb1_ok, 1)

            def w_lo(lo, raw, hi, n):
                pool.wait_ge(whi_ok, n)
                pool.tensor_tensor(lo, raw, hi.bitcast(f32), ALU.subtract).then_inc(wlo_ok, 1)

            def x_lo(g):
                pool.wait_ge(xH_ok, g + 1)
                pool.tensor_tensor(xL[:, bass.ds(g * T, T)], xn2T[:, :], xH[:, bass.ds(g * T, T)].bitcast(f32),
                                   ALU.subtract).then_inc(xL_ok, 1)

            def ln2_scales(g, count, first=False):
                if not first:
                    pool.wait_ge(xn2_ok, g * GB)
                pool.wait_ge(mv2_ok, g + 1)
                if not first:
                    pool.tensor_tensor(nm2[:, :], mv2[:, :, 0], minus1[:, :], ALU.mult)
                pool.tensor_tensor(ve2[:, :], mv2[:, :, 1], epsc[:, :], ALU.add).then_inc(pool_seq, 1)
                pool.wait_ge(pool_seq, count + 1)
                pool.tensor_tensor(rs2[:, :], ve2[:, :], mhalf[:, :], ALU.pow).then_inc(rs2_ok, 1)
                if not first:
                    pool.wait_ge(rs2_ok, g + 1)
                    pool.tensor_tensor(nb2[:, :], nm2[:, :], rs2[:, :], ALU.mult).then_inc(nb2_ok, 1)

            def sh_lo(g):
                pool.wait_ge(shaH_ok, g + 1)
                pool.tensor_tensor(sh_parts[0:M, :], sh_act[M:2 * M, :], sh_parts[M:2 * M, :].bitcast(f32),
                                   ALU.subtract).then_inc(shaL_ok, 1)
                pool.wait_ge(shaL_ok, g + 1)

            def act_lo(g, k):
                i = (k - 1) % ABUF
                pool.wait_ge(actH_ok, g * PAIRS + k)
                pool.tensor_tensor(actL[:, i], act[:, i], actH[:, i].bitcast(f32), ALU.subtract).then_inc(actL_ok, 1)

            w_lo(shL[:, :], shraw[:, :], shH[:, :], 1)
            chain_before = seq[0]
            ln2_scales(0, chain_before, True)
            w_lo(wL[:, 0], wraw[:, 0], wH[:, 0], 2)
            w_lo(wL[:, 1], wraw[:, 1], wH[:, 1], 3)
            ln2_scales(1, chain_before + 1)
            pool.wait_ge(nb2_ok, 1)
            sh_lo(0)
            w_lo(shdL[:, :], shd[:, :], shdH[:, :], 4)
            w_lo(wL[:, 2], wraw[:, 2], wH[:, 2], 5)

            def slots(g, nxt):
                for k in range(3, SLOTS):
                    act_lo(g, k - 2)
                    if nxt and k == 5:
                        ln2_scales(g + 2, chain_before + g + 2)
                    if nxt and k == 6:
                        x_lo(g + 1)
                if nxt:
                    act_lo(g, SLOTS - 2)
                    act_lo(g, SLOTS - 1)
                    pool.wait_ge(actL_ok, (g + 1) * PAIRS)
                    sh_lo(g + 1)

            with pool.Fori(0, NG - 1) as g:
                slots(g, True)
            slots(NG - 1, False)

        @block.scalar
        def _(a):
            a.wait_ge(warm_in, 1)
            a.activation(gel[0:C, 0, 0, 0:1], warm[0:C, 0:1], ACT.Gelu_apprx_tanh)

            def evac(g):
                a.wait_ge(xn1_ps, g + 1)
                a.copy(xn1T_v[g % 2], pG[g % 2][:, :].rearrange("h (b s) -> h b s", s=S)).then_inc(xn1T_ok, 1)

            def gelu(g):
                a.wait_ge(h_ps, g + 1)
                a.activation(gel_v[g % 2], pU[g % 2][0:C, :].rearrange("c (b s) -> c b s", s=S),
                             ACT.Gelu_apprx_tanh).then_inc(gel_ok, 1)

            def w_hi(hi, raw, loaded, transfers=1):
                a.wait_ge(loaded, 16 * transfers)
                a.copy(hi, raw).then_inc(whi_ok, 1)

            def ln2_apply(g, b0, b1):
                a.wait_ge(nb2_ok, g)
                for b in range(b0, b1):
                    a.activation(xn2[:, b, :], xs[:, bass.ds(g * GB + b, 1), :], ACT.Identity, bias=nb2[:, b:b + 1],
                                 scale=rs2[:, b:b + 1]).then_inc(xn2_ok, 1)

            def route_evac(g):
                a.wait_ge(rt_ps, g + 1)
                a.copy(routeT[:, :], pA[0:RPARTS * E, 0:T // 2].bitcast(bf16)).then_inc(rt_ok, 1)

            def ln2_evac(g):
                a.wait_ge(xn2_ps, g + 1)
                a.copy(xn2T[:, :], pA[:, :]).then_inc(xn2T_ok, 1)

            def x_hi(g):
                a.wait_ge(xn2T_ok, g + 1)
                a.copy(xH[:, bass.ds(g * T, T)], xn2T[:, :]).then_inc(xH_ok, 1)

            def logit_silus(g):
                a.wait_ge(logit_ok, g + 1)
                a.activation(logit_silu[:, :, :], logit_c[:, :, :], ACT.Silu).then_inc(lsilu_ok, 1)

            def silu(g, k, first=False):
                a.wait_ge(gate_ps, g * SLOTS + k + 1)
                if k == 0:
                    a.activation(sh_silu[M:2 * M, :], sh_bank(first)[0:M, :], ACT.Silu).then_inc(silu_ok, 1)
                else:
                    i = (k - 1) % 2
                    a.activation(silu_s[:, i], pG[i][:, :], ACT.Silu).then_inc(silu_ok, 1)

            def act_hi(g, k):
                i = (k - 1) % ABUF
                a.wait_ge(act_ok, g * PAIRS + k)
                a.copy(actH[:, i], act[:, i]).then_inc(actH_ok, 1)

            def sh_hi(g):
                a.wait_ge(gated_ok, g * SLOTS + 1)
                a.copy(sh_parts[M:2 * M, :], sh_act[M:2 * M, :]).then_inc(shaH_ok, 1)

            def y_copy(g):
                a.wait_ge(y_ps, g + 1)
                a.copy(yT[:, :], pY[:, :]).then_inc(yT_ok, 1)

            evac(0)
            w_hi(shH[:, :], shraw[:, :], ld_sh)
            w_hi(wH[:, 0], wraw[:, 0], ld_w[0])
            gelu(0)
            evac(1)
            a.wait_ge(nb1_ok, 1)
            for b in range(2 * GB, 3 * GB):
                a.activation(xn1[:, b, :], xs[:, b, :], ACT.Identity, bias=nb1[:, b:b + 1],
                             scale=rs1[:, b:b + 1]).then_inc(xn1a_ok, 1)
            gelu(1)
            evac(2)
            w_hi(wH[:, 1], wraw[:, 1], ld_w[1])
            gelu(2)
            evac(3)
            ln2_evac(0)
            x_hi(0)
            gelu(3)
            logit_silus(0)
            silu(0, 0, first=True)
            w_hi(shdH[:, :], shd[:, :], ld_shd, 2)
            silu(0, 1)
            sh_hi(0)
            silu(0, 2)
            route_evac(0)
            w_hi(wH[:, 2], wraw[:, 2], ld_w[2])

            def slots(g, nxt):
                for k in range(3, SLOTS):
                    if nxt and k == 3:
                        ln2_apply(g + 1, 0, GB // 2)
                    silu(g, k)
                    if nxt and k == 3:
                        ln2_apply(g + 1, GB // 2, GB)
                    if nxt and k == 4:
                        ln2_evac(g + 1)
                    if nxt and k == 6:
                        logit_silus(g + 1)
                    act_hi(g, k - 2)
                    if nxt and k == 5:
                        x_hi(g + 1)
                if nxt:
                    silu(g + 1, 0)
                    act_hi(g, SLOTS - 2)
                    route_evac(g + 1)
                    act_hi(g, SLOTS - 1)
                    silu(g + 1, 1)
                    sh_hi(g + 1)
                    silu(g + 1, 2)
                y_copy(g)

            with a.Fori(0, NG - 1) as g:
                slots(g, True)
            slots(NG - 1, False)

        @block.vector
        def _(v):
            seq = [0]

            def chain(ins, base=0):
                seq[0] += 1
                ins.then_inc(dve_seq, 1)
                v.wait_ge(dve_seq, base + seq[0])

            v.memset(warm[:, :], 0.0).then_inc(warm_in, 1)
            v.memset(rparts[:, :, :], 0.0)
            v.memset(score[:, :, E:SC], ABSENT)
            v.memset(top2[:, :, TOP:MAX8], ABSENT).then_inc(score_pad, 1)

            def ln_apply(dst, src, mv, rs):
                return v.tensor_scalar(dst, src, mv, rs, op0=ALU.subtract, op1=ALU.mult)

            def ln1_stats(b0, b1):
                for b in range(b0, b1):
                    if b == 0:
                        v.wait_ge(ld_x_half, 16)
                    elif b % GB == 0 or b == GB // 2:
                        v.wait_ge(ld_x[b // GB], 16)
                    last = v.bn_stats(st1[:, b, :], xs[:, b, :])
                chain(last)
                for b in range(b0, b1):
                    last = v.bn_aggr(mv1[:, b, :], st1[:, b, :])
                last.then_inc(mv1_ok, 1)

            def ln1_apply(g):
                v.wait_ge(mv1_ok, g + 1)
                v.wait_ge(rs1_ok, g + 1)
                for b in range(g * GB, (g + 1) * GB):
                    ln_apply(xn1[:, b, :], xs[:, b, :], mv1[:, b, 0:1], rs1[:, b:b + 1]).then_inc(xn1_ok, 1)

            ln1_stats(0, GB)
            ln1_stats(GB, 2 * GB)
            ln1_apply(0)
            ln1_stats(2 * GB, 3 * GB)
            ln1_apply(1)
            ln1_stats(3 * GB, B)

            def residual(g):
                v.wait_ge(att_ps, g + 1)
                sl = xs[:, g * GB:(g + 1) * GB, :]
                v.tensor_tensor(sl, pR[g % 2][:, :].rearrange("s (b h) -> s b h", h=H), sl,
                                ALU.add).then_inc(x1_ok, 1)

            def ln2_stats(g, ch):
                for b in range(GB):
                    last = v.bn_stats(st2[:, b, :], xs[:, bass.ds(g * GB + b, 1), :])
                ch(last)

            def ln2_aggregate():
                for b in range(GB):
                    last = v.bn_aggr(mv2[:, b, :], st2[:, b, :])
                last.then_inc(mv2_ok, 1)

            part0, part1, part2 = (rparts[:, :, c * E:(c + 1) * E] for c in range(RPARTS))

            def logit_bounds(g, ch):
                lg = pA[:, 0:GB * E].rearrange("s (b e) -> s b e", e=E)
                v.wait_ge(lg_ps, g + 1)
                ch(v.tensor_scalar(above[:, :, :], lg, -TINY, TINY, op0=ALU.is_gt, op1=ALU.mult))
                v.tensor_scalar(logit[:, :, :], lg, SATURATED, None, op0=ALU.min)
                ch(v.scalar_tensor_tensor(near0[:, :, :], lg, TINY, above[:, :, :],
                                          op0=ALU.is_lt, op1=ALU.mult))
                v.tensor_tensor(logit_c[:, :, :], near0[:, :, :], logit[:, :, :], ALU.add).then_inc(logit_ok, 1)

            def logit_reciprocals(g, ch):
                v.wait_ge(logit_ok, g + 1)
                ch(v.reciprocal(logit_r[:, :, :], logit_c[:, :, :]))

            def scores(g):
                v.wait_ge(lsilu_ok, g + 1)
                v.tensor_tensor(score[:, :, 0:E], logit_silu[:, :, :], logit_r[:, :, :],
                                ALU.mult).then_inc(score_ok, 1)

            def largest(g, ch):
                v.wait_ge(score_pad, 1)
                v.wait_ge(score_ok, g + 1)
                for b in range(GB):
                    last = v.max(top8[:, b, :], score[:, b, 0:E])
                ch(last)

            def first_two(ch):
                ch(v.tensor_copy(top2[:, :, 0:TOP], top8[:, :, 0:TOP]))
                v.scalar_tensor_tensor(rsum[:, :], top8[:, :, 0], TOPK_EPS, top8[:, :, 1],
                                       op0=ALU.add, op1=ALU.add)
                for b in range(GB):
                    last = v.match_replace(picked[:, b, :], top2[:, b, :], score[:, b, :], ABSENT)
                ch(last)

            def route_parts(ch):
                v.reciprocal(rinv[:, :], rsum[:, :])
                ch(v.scalar_tensor_tensor(r1[:, :, :], picked[:, :, 0:E], 0.0, score[:, :, 0:E],
                                          op0=ALU.is_lt, op1=ALU.mult))
                v.scalar_tensor_tensor(part0, r1[:, :, :], ROUTE_SCALE, bcast(rinv[:, :], E),
                                       op0=ALU.mult, op1=ALU.mult)
                ch(v.scalar_tensor_tensor(r2[:, :, :], r1[:, :, :], ROUTE_SCALE, bcast(rinv[:, :], E),
                                          op0=ALU.mult, op1=ALU.mult))
                v.tensor_tensor(part1, r2[:, :, :], part0, ALU.subtract)
                ch(v.tensor_tensor(r3[:, :, :], r2[:, :, :], part0, ALU.subtract))

            def route_last_part():
                v.tensor_tensor(part2, r3[:, :, :], part1, ALU.subtract).then_inc(rp_ok, 1)

            def gate_up(g, k, first=False):
                v.wait_ge(silu_ok, g * SLOTS + k + 1)
                if k == 0:
                    v.tensor_tensor(sh_act[M:2 * M, :], sh_bank(first)[M:2 * M, :], sh_silu[M:2 * M, :],
                                    ALU.mult).then_inc(gated_ok, 1)
                else:
                    i = (k - 1) % 2
                    v.wait_ge(up_ps, g * PAIRS + k)
                    v.tensor_tensor(gated[:, (k - 1) % GBUF], pU[i][:, :], silu_s[:, i],
                                    ALU.mult).then_inc(gated_ok, 1)

            def apply_route(g, k):
                i, j = (k - 1) % 2, (k - 1) % ABUF
                v.wait_ge(r_ps, g * PAIRS + k)
                v.wait_ge(gated_ok, g * SLOTS + k + 1)
                v.tensor_tensor(act[:, j], pR[i][:, :], gated[:, (k - 1) % GBUF], ALU.mult).then_inc(act_ok, 1)

            def out_add(g):
                v.wait_ge(yt_ps, g + 1)
                sl = xs[:, bass.ds(g * GB, GB), :]
                v.tensor_tensor(sl, pA[:, :].rearrange("s (b h) -> s b h", h=H), sl, ALU.add).then_inc(y_ok, 1)

            residual(0)
            v.wait_ge(x1_ok, 1)
            ln2_stats(0, chain)
            ln2_aggregate()
            ln1_apply(3)
            residual(1)
            v.wait_ge(mv2_ok, 1)
            v.wait_ge(rs2_ok, 1)
            for b in range(GB):
                ln_apply(xn2[:, b, :], xs[:, b, :], mv2[:, b, 0:1], rs2[:, b:b + 1]).then_inc(xn2_ok, 1)
            v.wait_ge(x1_ok, 2)
            v.wait_ge(xn2_ok, GB)
            ln2_stats(1, chain)
            ln2_aggregate()
            v.wait_ge(xH_ok, 1)
            v.tensor_tensor(xL[:, 0:T], xn2T[:, :], xH[:, 0:T].bitcast(f32), ALU.subtract).then_inc(xL_ok, 1)
            logit_bounds(0, chain)
            logit_reciprocals(0, chain)
            scores(0)
            residual(2)
            largest(0, chain)
            gate_up(0, 0, first=True)
            first_two(chain)
            route_parts(chain)
            route_last_part()
            residual(3)
            gate_up(0, 1)
            gate_up(0, 2)
            apply_route(0, 1)
            apply_route(0, 2)
            v.wait_ge(x1_ok, NG)
            v.wait_ge(pad_ok, 1)
            before = seq[0]
            PER = 10

            def slots(g, nxt):
                seq[0] = before

                def ch(ins):
                    chain(ins, g * PER)
                for k in range(3, SLOTS):
                    if k > 3:
                        apply_route(g, k - 1)
                    if nxt and k == 4:
                        ln2_stats(g + 2, ch)
                    if nxt and k == 6:
                        logit_reciprocals(g + 1, ch)
                    if nxt and k == 7:
                        largest(g + 1, ch)
                    if nxt and k == 8:
                        route_parts(ch)
                    gate_up(g, k)
                    if nxt and k == 4:
                        ln2_aggregate()
                    if nxt and k == 5:
                        logit_bounds(g + 1, ch)
                    if nxt and k == 6:
                        scores(g + 1)
                    if nxt and k == 7:
                        first_two(ch)
                    if nxt and k == 8:
                        route_last_part()
                if nxt:
                    assert seq[0] == before + PER, seq[0] - before
                    gate_up(g + 1, 0)
                apply_route(g, SLOTS - 1)
                if nxt:
                    gate_up(g + 1, 1)
                    gate_up(g + 1, 2)
                    apply_route(g + 1, 1)
                    apply_route(g + 1, 2)
                if nxt:
                    out_add(g)
                else:
                    for b in range(GB):
                        v.wait_ge(yt_ps, g + 1 + b)
                        sl = xs[:, g * GB + b, :]
                        last = v.tensor_tensor(sl, y_last[b][:, 0:H], sl, ALU.add)
                        if b % HB == HB - 1:
                            last.then_inc(y_ok, 1)

            with v.Fori(0, NG - 1) as g:
                slots(g, True)
            slots(NG - 1, False)

        @block.tensor
        def _(pe):
            def transposes1(g):
                if g >= 2:
                    pe.wait_ge(xn1T_ok, g - 1)
                for b in range(GB):
                    if g == 2:
                        pe.wait_ge(xn1a_ok, b + 1)
                    else:
                        pe.wait_ge(xn1_ok, (g if g < 2 else 2) * GB + b + 1)
                    last = pe.transpose(pG[g % 2][:, b * S:(b + 1) * S], xn1[:, g * GB + b, :], identf[:, :])
                last.then_inc(xn1_ps, 1)

            def attend(g):
                if g <= 1:
                    pe.wait_ge(ld_ct if g else ld_ct0, 16)
                pe.wait_ge(xn1T_ok, g + 1)
                if g >= 2:
                    pe.wait_ge(gel_ok, g - 1)
                for b in range(GB):
                    last = pe.matmul(pU[g % 2][0:C, b * S:(b + 1) * S], csT[:, g * GB + b, :],
                                     xn1T_v[g % 2][:, b, :], start=True, stop=True)
                last.then_inc(h_ps, 1)

            def attend_out(g):
                if g <= 1:
                    pe.wait_ge(ld_c if g else ld_c0, 16)
                pe.wait_ge(gel_ok, g + 1)
                if g >= 2:
                    pe.wait_ge(x1_ok, g - 1)
                for b in range(GB):
                    last = pe.matmul(pR[g % 2][:, b * H:(b + 1) * H], gel_v[g % 2][:, b, :], cs[:, g * GB + b, :],
                                     start=True, stop=True)
                last.then_inc(att_ps, 1)

            def ln2_transposes(g, before=None):
                if before is not None:
                    pe.wait_ge(gated_ok, before * SLOTS + 4)
                for b in range(GB):
                    pe.wait_ge(xn2_ok, g * GB + b + 1)
                    last = pe.transpose(pA[:, b * S:(b + 1) * S], xn2[:, b, :], identf[:, :])
                last.then_inc(xn2_ps, 1)

            def logits(g):
                pe.wait_ge(xn2T_ok, g + 1)
                for b in range(GB):
                    last = pe.matmul(pA[:, b * E:(b + 1) * E], xn2T[:, b * S:(b + 1) * S], gwT[:, :],
                                     start=True, stop=True)
                last.then_inc(lg_ps, 1)

            def route_transposes(g):
                pe.wait_ge(rp_ok, g + 1)
                pAb = pA[:, 0:T // 2].bitcast(bf16)
                for b in range(GB):
                    last = pe.transpose(pAb[:, b * S:(b + 1) * S], rparts[:, b, :], identb[:, :])
                last.then_inc(rt_ps, 1)

            def three(dst, hi, lo, g):
                th, tl = xH[:, bass.ds(g * T, T)], xL[:, bass.ds(g * T, T)]
                pe.matmul(dst, hi, th, start=True, stop=False)
                pe.matmul(dst, hi, tl, start=False, stop=False)
                return pe.matmul(dst, lo, th, start=False, stop=True)

            def shared_products(g, first=False):
                if not first:
                    pe.wait_ge(gated_ok, g * SLOTS - 1)
                pe.wait_ge(xL_ok, g + 1)
                three(sh_bank(first)[:, :], shH[:, :], shL[:, :], g).then_inc(gate_ps, 1)

            def gate_products(g, k, first=False):
                c0 = (k - 1) * 2 * M
                if k >= 2 and not first:
                    pe.wait_ge(gated_ok, g * SLOTS + k - 1)
                three(pG[(k - 1) % 2][:, :], wH[:, 0, c0:c0 + 2 * M], wL[:, 0, c0:c0 + 2 * M], g).then_inc(gate_ps, 1)

            def up_products(g, k):
                c0 = (k - 1) * 2 * M
                three(pU[(k - 1) % 2][:, :], wH[:, 1, c0:c0 + 2 * M], wL[:, 1, c0:c0 + 2 * M], g).then_inc(up_ps, 1)

            def spread_route(g, k, first=False):
                if k == 1:
                    pe.wait_ge(rt_ok, g + 1)
                if first:
                    pe.wait_ge(x1_ok, NG - 2 + k)
                else:
                    pe.wait_ge(act_ok, g * PAIRS + k - 2)
                pe.matmul(pR[(k - 1) % 2][:, :], spread[:, k - 1].rearrange("e a m -> e (a m)"), routeT[:, :],
                          start=True, stop=True).then_inc(r_ps, 1)

            def down_shared(g):
                pe.wait_ge(wlo_ok, 4)
                pe.wait_ge(shaL_ok, g + 1)
                pe.matmul(pY[:, :], shdH[:, :], sh_parts[:, :], start=True, stop=False)
                pe.matmul(pY[:, :], shdL[M:2 * M, :], sh_parts[M:2 * M, :], start=False, stop=False)

            def down_hi(g, k):
                i, c0 = (k - 1) % ABUF, (k - 1) * H
                if k == 1:
                    pe.wait_ge(wlo_ok, 5)
                pe.wait_ge(actH_ok, g * PAIRS + k)
                pe.matmul(pY[:, :], wH[:, 2, c0:c0 + H], actH[:, i], start=False, stop=False)
                pe.matmul(pY[:, :], wL[:, 2, c0:c0 + H], actH[:, i], start=False, stop=False)

            def down_lo(g, k, ends=False):
                i, c0 = (k - 1) % ABUF, (k - 1) * H
                pe.wait_ge(actL_ok, g * PAIRS + k)
                last = pe.matmul(pY[:, :], wH[:, 2, c0:c0 + H], actL[:, i], start=False, stop=ends)
                if ends:
                    last.then_inc(y_ps, 1)

            def down(g, k):
                if k == 0:
                    down_shared(g)
                else:
                    down_hi(g, k)
                    down_lo(g, k, ends=(k == SLOTS - 1))

            def down_direct(g, k):
                i, c0 = (k - 1) % ABUF, (k - 1) * H
                pe.wait_ge(act_ok, g * PAIRS + k)
                pe.matmul(pY[:, :], wraw[:, 2, c0:c0 + H], act[:, i], start=False, stop=False)

            def last_output(g):
                k = SLOTS - 1
                i, c0 = (k - 1) % ABUF, (k - 1) * H
                pe.wait_ge(act_ok, g * PAIRS + k)
                for b in range(GB):
                    pe.matmul(y_last[b][:, 0:H], act[:, i, b * S:(b + 1) * S], wraw[:, 2, c0:c0 + H], start=True,
                              stop=False)
                pe.wait_ge(yT_ok, g + 1)
                for b in range(GB):
                    pe.matmul(y_last[b][:, 0:H], yT[:, b * S:(b + 1) * S], identf[:, :], start=False,
                              stop=True).then_inc(yt_ps, 1)

            def out_transposes(g):
                pe.wait_ge(yT_ok, g + 1)
                for b in range(GB):
                    last = pe.transpose(pA[:, b * H:(b + 1) * H], yT[:, b * S:(b + 1) * S], identf[:, :])
                last.then_inc(yt_ps, 1)

            zero16 = warm[:, :].bitcast(bf16)

            def keep_warm(n):
                for _ in range(n):
                    pe.matmul(pY[:, :], zero16[:, 0:128], zero16, start=True, stop=True)

            pe.wait_ge(warm_in, 1)
            keep_warm(WARM[0])
            pe.wait_ge(ld_eye, 16)
            transposes1(0)
            keep_warm(WARM[1])
            attend(0)
            transposes1(1)
            keep_warm(WARM[2])
            attend_out(0)
            attend(1)
            keep_warm(WARM[3])
            transposes1(2)
            attend_out(1)
            attend(2)
            transposes1(3)
            ln2_transposes(0)
            attend(3)
            pe.wait_ge(ld_gw, 16)
            logits(0)
            attend_out(2)
            keep_warm(WARM[4])
            pe.wait_ge(wlo_ok, 1)
            pe.wait_ge(gel_ok, NG)
            shared_products(0, first=True)
            pe.wait_ge(wlo_ok, 3)
            gate_products(0, 1, first=True)
            up_products(0, 1)
            attend_out(3)
            gate_products(0, 2, first=True)
            pe.wait_ge(gated_ok, 1)
            up_products(0, 2)
            pe.wait_ge(ld_eye16, 16)
            keep_warm(WARM[5])
            route_transposes(0)
            keep_warm(WARM[6])
            pe.wait_ge(ld_spread, 16)
            spread_route(0, 1, first=True)
            spread_route(0, 2, first=True)

            def slots(g, nxt):
                for k in range(3, SLOTS):
                    gate_products(g, k)
                    if nxt and k == 5:
                        logits(g + 1)
                    up_products(g, k)
                    if nxt and k == 4:
                        ln2_transposes(g + 1, g)
                    if k >= LAG:
                        down(g, k - LAG)
                    spread_route(g, k)
                if nxt:
                    shared_products(g + 1)
                    down(g, SLOTS - LAG)
                    gate_products(g + 1, 1)
                    route_transposes(g + 1)
                    down(g, SLOTS - 3)
                    pe.wait_ge(gated_ok, (g + 1) * SLOTS + 1)
                    up_products(g + 1, 1)
                    down(g, SLOTS - 2)
                    spread_route(g + 1, 1)
                    gate_products(g + 1, 2)
                    down(g, SLOTS - 1)
                    up_products(g + 1, 2)
                    spread_route(g + 1, 2)
                    out_transposes(g)
                else:
                    down(g, SLOTS - LAG)
                    down_hi(g, SLOTS - 3)
                    down_direct(g, SLOTS - 2)
                    down_lo(g, SLOTS - 3, ends=True)
                    last_output(g)

            with pe.Fori(0, NG - 1) as g:
                slots(g, True)
            slots(NG - 1, False)


def kernel(x, ctx_1024, L0_ffn_gate_w, L0_ffn_w_gate, L0_ffn_w_up, L0_ffn_w_down, L0_ffn_ws_gate, L0_ffn_ws_up,
           L0_ffn_ws_down):
    import ml_dtypes
    import numpy as np
    import concourse.bacc as bacc
    from concourse import mybir as mb
    from concourse.bass_utils import run_bass_kernel_spmd

    x, ctx = np.asarray(x), np.asarray(ctx_1024)
    w_gate, w_up, w_down = (np.asarray(w) for w in (L0_ffn_w_gate, L0_ffn_w_up, L0_ffn_w_down))
    E, H, M = w_gate.shape
    PARTS = 3
    spread01 = np.tile(np.repeat(np.eye(E), M, axis=1), (PARTS, 1)).reshape(PARTS * E, E // 2, 2, M)
    laid_out = {
        "x": x.transpose(1, 0, 2),
        "ctx_kv": ctx.transpose(1, 0, 2),
        "ctx_t": ctx.transpose(2, 0, 1),
        "gate_t": np.asarray(L0_ffn_gate_w).T,
        "w_gate": w_gate.transpose(1, 0, 2).reshape(H, E * M),
        "w_up": w_up.transpose(1, 0, 2).reshape(H, E * M),
        "w_down": w_down.reshape(E // 2, 2 * M, H).transpose(1, 0, 2).reshape(2 * M, E // 2 * H),
        "ws_gu": np.concatenate([np.asarray(L0_ffn_ws_gate), np.asarray(L0_ffn_ws_up)], axis=1),
        "ws_down": np.asarray(L0_ffn_ws_down),
        "eye": np.eye(128, dtype=np.float32),
        "eye16": np.eye(128).astype(ml_dtypes.bfloat16),
        "spread01": spread01.astype(ml_dtypes.bfloat16),
    }
    nc = bacc.Bacc("TRN2", target_bir_lowering=False, num_devices=1)
    arrays, args = {}, []
    for name, a in laid_out.items():
        a = np.ascontiguousarray(a)
        arrays[f"in_{name}"] = a
        args.append(nc.dram_tensor(f"in_{name}", a.shape, mb.dt.from_np(a.dtype), kind="ExternalInput").ap())
    B, S, _ = x.shape
    args.append(nc.dram_tensor("out_dram", (S, B, H), mb.dt.float32, kind="ExternalOutput").ap())
    xattn_moe_kernel(nc, *args)
    r = run_bass_kernel_spmd(nc, [arrays], core_ids=[0])
    return r.results[0]["out_dram"].transpose(1, 0, 2)
```
